# Optimizing a Trainium2 kernel written in Bass

```python
import numpy as np
import jax
import jax.numpy as jnp

def _softmax(x, axis=-1):
    return jax.nn.softmax(x, axis=axis)

def _gelu(x):
    return jax.nn.gelu(x, approximate=True)

def _silu(x):
    return jax.nn.silu(x)

def _sigmoid(x):
    return jax.nn.sigmoid(x)

def _layernorm(x, axis=-1, eps=1e-05):
    m = jnp.mean(x, axis=axis, keepdims=True)
    v = jnp.var(x, axis=axis, keepdims=True)
    return (x - m) / jnp.sqrt(v + eps)

def _scatter_add(tgt, idx, src, axis=0):
    return tgt.at[idx].add(src)

def _segment_sum(src, seg, n):
    return jax.ops.segment_sum(src, seg, n)
kernel_name = 'mk_xattn_seq_d2_seqx_r2_b4c051'

def setup_inputs(seed: int=0):
    np.random.seed(seed)
    _w = jnp.asarray

    def _rec_inputs():
        import jax
        import jax.numpy as jnp
        _rk = jax.random.key(seed)
        x = -0.0002928 + 1 * jax.random.normal(jax.random.fold_in(_rk, 1), (4, 1024, 512), jnp.float32)
        _lenS = 1024 - jax.random.randint(jax.random.fold_in(_rk, 7), (4,), 0, max(1, 1024 // 4) + 1, jnp.int32)
        _lenS2 = 64 - jax.random.randint(jax.random.fold_in(_rk, 8), (4,), 0, max(1, 64 // 4) + 1, jnp.int32)
        _ctx_1024P = jax.random.normal(jax.random.fold_in(_rk, 11), (4, 16, 512), jnp.float32)
        _ctx_1024c = jax.random.dirichlet(jax.random.fold_in(_rk, 511), 0.3 * jnp.ones((16,), jnp.float32), (4, 64))
        _ctx_1024t = jnp.einsum('bsk,bkd->bsd', _ctx_1024c, _ctx_1024P)
        _ctx_1024t = _ctx_1024t * jax.lax.rsqrt(jnp.mean(jnp.square(_ctx_1024t)) + 1e-12) * 0.953939
        ctx_1024 = -1.39393e-06 + 0.999914 * (_ctx_1024t + 0.3 * jax.random.normal(jax.random.fold_in(_rk, 611), (4, 64, 512), jnp.float32))
        return (x, ctx_1024)
    x, ctx_1024 = _rec_inputs()

    def _L0_xattn_setup():
        import jax, jax.numpy as jnp
        import numpy as np
        B, T, TE, C, H = (2, 1024, 1024, 512, 16)
        DH = C // H
        EPS = 1e-05

        def _ln(x, g, b):
            mu = jnp.mean(x, axis=-1, keepdims=True)
            var = jnp.mean((x - mu) ** 2, axis=-1, keepdims=True)
            return (x - mu) * jax.lax.rsqrt(var + EPS) * g + b

        def _mha(xn, kv_src, Wq, bq, Wk, bk, Wv, bv, causal):
            q = jnp.einsum('btc,hcd->bhtd', xn, Wq) + bq[None, :, None, :]
            k = jnp.einsum('bsc,hcd->bhsd', kv_src, Wk) + bk[None, :, None, :]
            v = jnp.einsum('bsc,hcd->bhsd', kv_src, Wv) + bv[None, :, None, :]
            scale = DH ** (-0.5)
            scores = jnp.einsum('bhtd,bhsd->bhts', q, k) / scale
            if causal:
                Tq, Ts = (scores.shape[-2], scores.shape[-1])
                mask = jnp.tril(jnp.ones((Tq, Ts), dtype=bool))
                scores = jnp.where(mask[None, None], scores, -jnp.inf)
            attn = jax.nn.softmax(scores, axis=-1)
            out = jnp.einsum('bhts,bhsd->bhtd', attn, v)
            b_, h_, t_, d_ = out.shape
            return out.transpose(0, 2, 1, 3).reshape(b_, t_, h_ * d_)
        key = jax.random.key(seed)
        ks = jax.random.split(key, 24)
        s = 0.02
        d = {'x': jax.random.normal(ks[0], (B, T, C), jnp.float32), 'encoder_out': jax.random.normal(ks[1], (B, TE, C), jnp.float32), 'Wq_s': jax.random.normal(ks[2], (H, C, DH)) * s, 'bq_s': jnp.zeros((H, DH)), 'Wk_s': jax.random.normal(ks[3], (H, C, DH)) * s, 'bk_s': jnp.zeros((H, DH)), 'Wv_s': jax.random.normal(ks[4], (H, C, DH)) * s, 'bv_s': jnp.zeros((H, DH)), 'W1': jax.random.normal(ks[5], (C, C)) * s, 'b1': jnp.zeros((C,)), 'g1': jnp.ones((C,)), 'be1': jnp.zeros((C,)), 'Wq_c': jax.random.normal(ks[6], (H, C, DH)) * s, 'bq_c': jnp.zeros((H, DH)), 'Wk_c': jax.random.normal(ks[7], (H, C, DH)) * s, 'bk_c': jnp.zeros((H, DH)), 'Wv_c': jax.random.normal(ks[8], (H, C, DH)) * s, 'bv_c': jnp.zeros((H, DH)), 'W2': jax.random.normal(ks[9], (C, C)) * s, 'b2': jnp.zeros((C,)), 'g2': jnp.ones((C,)), 'be2': jnp.zeros((C,)), 'g3': jnp.ones((C,)), 'be3': jnp.zeros((C,)), 'Wf1': jax.random.normal(ks[10], (C, 4 * C)) * s, 'bf1': jnp.zeros((4 * C,)), 'Wf2': jax.random.normal(ks[11], (4 * C, C)) * s, 'bf2': jnp.zeros((C,))}
        return d
    _L0_xattn_all = _L0_xattn_setup()
    _L0_xattn_in = {k: v for k, v in _L0_xattn_all.items() if k in ('Wq_s', 'bq_s', 'Wk_s', 'bk_s', 'Wv_s', 'bv_s', 'W1', 'b1', 'g1', 'be1', 'Wq_c', 'bq_c', 'Wk_c', 'bk_c', 'Wv_c', 'bv_c', 'W2', 'b2', 'g2', 'be2', 'g3', 'be3', 'Wf1', 'bf1', 'Wf2', 'bf2')}
    del _L0_xattn_all

    def _L1_xattn_setup():
        import jax, jax.numpy as jnp
        import numpy as np
        NUM_ITERATIONS = 3
        LN_EPS = 1e-05
        key = jax.random.key(seed)
        ks = jax.random.split(key, 10)
        B, L, Lv, H = (8, 1024, 128, 512)
        s = 1.0 / np.sqrt(H)
        s2 = 1.0 / np.sqrt(2 * H)
        return {'text_feat': jax.random.normal(ks[0], (B, L, H), dtype=jnp.float32), 'vision_feat': jax.random.normal(ks[1], (B, Lv, H), dtype=jnp.float32), 'Wt': jax.random.uniform(ks[2], (H, H), jnp.float32, -s, s), 'bt': jax.random.uniform(ks[3], (H,), jnp.float32, -s, s), 'Wv': jax.random.uniform(ks[4], (H, H), jnp.float32, -s, s), 'bv': jax.random.uniform(ks[5], (H,), jnp.float32, -s, s), 'Wg': jax.random.uniform(ks[6], (H, 2 * H), jnp.float32, -s2, s2), 'bg': jax.random.uniform(ks[7], (H,), jnp.float32, -s2, s2), 'gamma': jnp.ones((H,), jnp.float32), 'beta': jnp.zeros((H,), jnp.float32)}
    _L1_xattn_all = _L1_xattn_setup()
    _L1_xattn_in = {k: v for k, v in _L1_xattn_all.items() if k in ('Wt', 'bt', 'Wv', 'bv', 'Wg', 'bg', 'gamma', 'beta')}
    del _L1_xattn_all
    return {'x': x, 'ctx_1024': ctx_1024, 'L0_xattn_Wq_s': _L0_xattn_in['Wq_s'], 'L0_xattn_bq_s': _L0_xattn_in['bq_s'], 'L0_xattn_Wk_s': _L0_xattn_in['Wk_s'], 'L0_xattn_bk_s': _L0_xattn_in['bk_s'], 'L0_xattn_Wv_s': _L0_xattn_in['Wv_s'], 'L0_xattn_bv_s': _L0_xattn_in['bv_s'], 'L0_xattn_W1': _L0_xattn_in['W1'], 'L0_xattn_b1': _L0_xattn_in['b1'], 'L0_xattn_g1': _L0_xattn_in['g1'], 'L0_xattn_be1': _L0_xattn_in['be1'], 'L0_xattn_Wq_c': _L0_xattn_in['Wq_c'], 'L0_xattn_bq_c': _L0_xattn_in['bq_c'], 'L0_xattn_Wk_c': _L0_xattn_in['Wk_c'], 'L0_xattn_bk_c': _L0_xattn_in['bk_c'], 'L0_xattn_Wv_c': _L0_xattn_in['Wv_c'], 'L0_xattn_bv_c': _L0_xattn_in['bv_c'], 'L0_xattn_W2': _L0_xattn_in['W2'], 'L0_xattn_b2': _L0_xattn_in['b2'], 'L0_xattn_g2': _L0_xattn_in['g2'], 'L0_xattn_be2': _L0_xattn_in['be2'], 'L0_xattn_g3': _L0_xattn_in['g3'], 'L0_xattn_be3': _L0_xattn_in['be3'], 'L0_xattn_Wf1': _L0_xattn_in['Wf1'], 'L0_xattn_bf1': _L0_xattn_in['bf1'], 'L0_xattn_Wf2': _L0_xattn_in['Wf2'], 'L0_xattn_bf2': _L0_xattn_in['bf2'], 'L1_xattn_Wt': _L1_xattn_in['Wt'], 'L1_xattn_bt': _L1_xattn_in['bt'], 'L1_xattn_Wv': _L1_xattn_in['Wv'], 'L1_xattn_bv': _L1_xattn_in['bv'], 'L1_xattn_Wg': _L1_xattn_in['Wg'], 'L1_xattn_bg': _L1_xattn_in['bg'], 'L1_xattn_gamma': _L1_xattn_in['gamma'], 'L1_xattn_beta': _L1_xattn_in['beta']}

def reference(x, ctx_1024, L0_xattn_Wq_s, L0_xattn_bq_s, L0_xattn_Wk_s, L0_xattn_bk_s, L0_xattn_Wv_s, L0_xattn_bv_s, L0_xattn_W1, L0_xattn_b1, L0_xattn_g1, L0_xattn_be1, L0_xattn_Wq_c, L0_xattn_bq_c, L0_xattn_Wk_c, L0_xattn_bk_c, L0_xattn_Wv_c, L0_xattn_bv_c, L0_xattn_W2, L0_xattn_b2, L0_xattn_g2, L0_xattn_be2, L0_xattn_g3, L0_xattn_be3, L0_xattn_Wf1, L0_xattn_bf1, L0_xattn_Wf2, L0_xattn_bf2, L1_xattn_Wt, L1_xattn_bt, L1_xattn_Wv, L1_xattn_bv, L1_xattn_Wg, L1_xattn_bg, L1_xattn_gamma, L1_xattn_beta):
    import jax
    import jax.numpy as jnp

    def _L0_xattn_ref(x, encoder_out, Wq_s, bq_s, Wk_s, bk_s, Wv_s, bv_s, W1, b1, g1, be1, Wq_c, bq_c, Wk_c, bk_c, Wv_c, bv_c, W2, b2, g2, be2, g3, be3, Wf1, bf1, Wf2, bf2):
        import jax, jax.numpy as jnp
        import numpy as np
        B, T, TE, C, H = (2, 1024, 1024, 512, 16)
        DH = C // H
        EPS = 1e-05

        def _ln(x, g, b):
            mu = jnp.mean(x, axis=-1, keepdims=True)
            var = jnp.mean((x - mu) ** 2, axis=-1, keepdims=True)
            return (x - mu) * jax.lax.rsqrt(var + EPS) * g + b

        def _mha(xn, kv_src, Wq, bq, Wk, bk, Wv, bv, causal):
            q = jnp.einsum('btc,hcd->bhtd', xn, Wq) + bq[None, :, None, :]
            k = jnp.einsum('bsc,hcd->bhsd', kv_src, Wk) + bk[None, :, None, :]
            v = jnp.einsum('bsc,hcd->bhsd', kv_src, Wv) + bv[None, :, None, :]
            scale = DH ** (-0.5)
            scores = jnp.einsum('bhtd,bhsd->bhts', q, k) / scale
            if causal:
                Tq, Ts = (scores.shape[-2], scores.shape[-1])
                mask = jnp.tril(jnp.ones((Tq, Ts), dtype=bool))
                scores = jnp.where(mask[None, None], scores, -jnp.inf)
            attn = jax.nn.softmax(scores, axis=-1)
            out = jnp.einsum('bhts,bhsd->bhtd', attn, v)
            b_, h_, t_, d_ = out.shape
            return out.transpose(0, 2, 1, 3).reshape(b_, t_, h_ * d_)
        xn1 = _ln(x, g1, be1)
        sa = _mha(xn1, xn1, Wq_s, bq_s, Wk_s, bk_s, Wv_s, bv_s, causal=True)
        x = x + (sa @ W1 + b1)
        xn2 = _ln(x, g2, be2)
        ca = _mha(xn2, encoder_out, Wq_c, bq_c, Wk_c, bk_c, Wv_c, bv_c, causal=False)
        x = x + (ca @ W2 + b2)
        xn3 = _ln(x, g3, be3)
        ff = jax.nn.relu(xn3 @ Wf1 + bf1) @ Wf2 + bf2
        return x + ff

    def _L1_xattn_ref(text_feat, vision_feat, Wt, bt, Wv, bv, Wg, bg, gamma, beta):
        import jax, jax.numpy as jnp
        import numpy as np
        NUM_ITERATIONS = 3
        LN_EPS = 1e-05
        B, L, H = text_feat.shape
        vision_pooled = jnp.mean(vision_feat, axis=1, keepdims=True)
        text_proj = jnp.einsum('blh,oh->blo', text_feat, Wt) + bt
        vision_proj = jnp.einsum('bkh,oh->bko', vision_pooled, Wv) + bv
        vision_proj = jnp.broadcast_to(vision_proj, (B, L, H))
        agreement = jnp.sum(text_proj * vision_proj, axis=-1, keepdims=True)
        coupling = jnp.zeros((B, L, 1), dtype=text_feat.dtype)
        fused = text_feat
        for _ in range(NUM_ITERATIONS):
            routing_weights = jax.nn.softmax(coupling, axis=1)
            weighted_vision = routing_weights * vision_proj
            Wg_t, Wg_v = (Wg[:, :H], Wg[:, H:])
            gate_pre = jnp.einsum('blh,oh->blo', text_proj, Wg_t) + jnp.einsum('blh,oh->blo', weighted_vision, Wg_v) + bg
            gate = jax.nn.sigmoid(gate_pre)
            fused = text_feat + gate * weighted_vision
            coupling = coupling + agreement
        mu = jnp.mean(fused, axis=-1, keepdims=True)
        var = jnp.mean(jnp.square(fused - mu), axis=-1, keepdims=True)
        out = (fused - mu) / jnp.sqrt(var + LN_EPS) * gamma + beta
        return out
    x = _L0_xattn_ref(x, ctx_1024, L0_xattn_Wq_s, L0_xattn_bq_s, L0_xattn_Wk_s, L0_xattn_bk_s, L0_xattn_Wv_s, L0_xattn_bv_s, L0_xattn_W1, L0_xattn_b1, L0_xattn_g1, L0_xattn_be1, L0_xattn_Wq_c, L0_xattn_bq_c, L0_xattn_Wk_c, L0_xattn_bk_c, L0_xattn_Wv_c, L0_xattn_bv_c, L0_xattn_W2, L0_xattn_b2, L0_xattn_g2, L0_xattn_be2, L0_xattn_g3, L0_xattn_be3, L0_xattn_Wf1, L0_xattn_bf1, L0_xattn_Wf2, L0_xattn_bf2)
    x = _L1_xattn_ref(x, ctx_1024, L1_xattn_Wt, L1_xattn_bt, L1_xattn_Wv, L1_xattn_bv, L1_xattn_Wg, L1_xattn_bg, L1_xattn_gamma, L1_xattn_beta)
    return x

_drawn_inputs = setup_inputs


def setup_inputs(seed=0):
    import zlib

    import numpy as np

    out = dict(_drawn_inputs(seed))
    spreads = {'L0_xattn_bq_s': (0.0, 0.1),
     'L0_xattn_bk_s': (0.0, 2.0),
     'L0_xattn_bv_s': (0.0, 0.1),
     'L0_xattn_b1': (0.0, 0.1),
     'L0_xattn_g1': (1.0, 0.2),
     'L0_xattn_be1': (0.0, 0.1),
     'L0_xattn_bq_c': (0.0, 0.1),
     'L0_xattn_bk_c': (0.0, 2.0),
     'L0_xattn_bv_c': (0.0, 0.1),
     'L0_xattn_b2': (0.0, 0.1),
     'L0_xattn_g2': (1.0, 0.2),
     'L0_xattn_be2': (0.0, 0.1),
     'L0_xattn_g3': (1.0, 0.2),
     'L0_xattn_be3': (0.0, 0.307),
     'L0_xattn_bf1': (0.0, 0.1),
     'L0_xattn_bf2': (0.0, 0.1),
     'L1_xattn_gamma': (1.0, 0.2),
     'L1_xattn_beta': (0.0, 0.1)}
    factors = {'L1_xattn_Wt': 8.0,
     'L1_xattn_bt': 64.0,
     'L1_xattn_Wv': 8.0,
     'L1_xattn_bv': 64.0,
     'L1_xattn_Wg': 24.307,
     'L1_xattn_bg': 64.0}
    for name, (base, spread) in spreads.items():
        noise = np.random.default_rng([zlib.crc32(name.encode()), seed]).standard_normal(out[name].shape)
        drawn = base * np.exp(spread * noise) if base else spread * noise
        out[name] = jnp.asarray(drawn.astype(out[name].dtype))
    for name, factor in factors.items():
        out[name] = (out[name] * factor).astype(out[name].dtype)
    return out
```

```python
import numpy as np
import concourse.bass as bass
from concourse import mybir
from contextlib import ExitStack

F32 = mybir.dt.float32
F32R = mybir.dt.float32r
BF16 = mybir.dt.bfloat16
ALU = mybir.AluOpType
ACT = mybir.ActivationFunctionType
AX = mybir.AxisListType.X

NB, T, C, H, DH = 4, 1024, 512, 16, 32
S = 64
KT = 4
EPS = 1e-5
SCALE = 1.0 / (DH ** -0.5)
NEG = -1e30


class Queue:

    def __init__(self, sem):
        self.sem, self.n, self.items, self.seen = sem, 0, [], {}

    def wait(self, *tokens):
        for t in tokens:
            if isinstance(t, list):
                self.wait(*t)
            elif t is not None and self.seen.get(id(t[0]), 0) < t[1]:
                self.seen[id(t[0])] = t[1]
                self.items.append((None, t[0], t[1]))

    def op(self, fn, *tokens, inc=True):
        self.wait(*tokens)
        if not inc:
            self.items.append((fn, None, 0))
            return None
        self.n += 1
        self.items.append((fn, self.sem, 1))
        return (self.sem, self.n)

    def dma(self, lane, out, in_, *tokens):
        self.wait(*tokens)
        lane[1] += 16
        self.items.append((lambda e, o=out, i=in_: e.dma_start(o, i), lane[0], 16))
        return (lane[0], lane[1])

    def last(self):
        return (self.sem, self.n)

    def play(self, eng):
        for fn, sem, n in self.items:
            if fn is None:
                eng.wait_ge(sem, n)
            elif sem is None:
                fn(eng)
            else:
                fn(eng).then_inc(sem, n)


class Banks:

    def __init__(self, aps, group=1):
        self.aps, self.free, self.at = aps, [[] for _ in aps], 0

    def take(self):
        i = self.at % len(self.aps)
        self.at += 1
        return i, self.aps[i], self.free[i]


def merge(a, b, ta, tb):
    done = [0.0, 0.0]
    live = [a, b]
    while live[0] or live[1]:
        i = 0 if live[1] is None or (live[0] is not None and done[0] / ta <= done[1] / tb) else 1
        cost = next(live[i], None)
        if cost is None:
            live[i] = None
        else:
            done[i] += cost


def window(gens, lag, width=2):
    live = []
    gens = list(gens)
    while gens or live:
        if gens and (not live or (len(live) < width and live[-1][1] >= lag)):
            live.append([gens.pop(0), 0])
        for g in list(live):
            g[1] += 1
            if next(g[0], StopIteration) is StopIteration:
                live.remove(g)


def program(nc, A, out):
    top = ExitStack()
    with top:
        sem = lambda n: top.enter_context(nc.semaphore(n))
        pe, act, dve, pool, sp = [Queue(sem(n)) for n in ("s_pe", "s_act", "s_dve", "s_pool", "s_sp")]
        engines = [pe, act, dve, pool]
        lanes = {}

        def lane(name):
            if name not in lanes:
                lanes[name] = [sem("d_" + name), 0]
            return lanes[name]

        def sb(ctx, name, shape, dt=F32):
            return ctx.enter_context(nc.sbuf_tensor(name, shape, dt))

        psum = top.enter_context(nc.psum_tensor("psum", [128, 8, 512], F32))
        bank = [psum[:, i, :] for i in range(8)]

        sa_d = nc.dram_tensor("sa_d", [C, NB * T], F32, kind="Internal").ap()
        x2_d = nc.dram_tensor("x2_d", [NB * T, C], F32, kind="Internal").ap()
        x3_d = nc.dram_tensor("x3_d", [NB * T, C], F32, kind="Internal").ap()
        wh_d = nc.dram_tensor("wh_d", [C, C], F32, kind="Internal").ap()
        wl_d = nc.dram_tensor("wl_d", [C, C], F32, kind="Internal").ap()
        vp_d = nc.dram_tensor("vp_d", [NB, C], F32, kind="Internal").ap()
        wvp_d = nc.dram_tensor("wvp_d", [NB, C], F32, kind="Internal").ap()
        u_d = nc.dram_tensor("u_d", [NB, C], F32, kind="Internal").ap()
        gb_d = nc.dram_tensor("gb_d", [1, C], F32, kind="Internal").ap()
        cb_d = nc.dram_tensor("cb_d", [NB, 1], F32, kind="Internal").ap()
        x_d = A["x"].rearrange("b t c -> (b t) c")
        out_d = out.rearrange("b t c -> (b t) c")
        stores = {}

        ident = sb(top, "ident", [128, 128])
        identb = sb(top, "identb", [128, 128], BF16)
        mask_ts = sb(top, "mask_ts", [128, 128], BF16)
        mask_st = sb(top, "mask_st", [128, 128], BF16)
        cols = sb(top, "cols", [128, 68])
        small = sb(top, "small", [128, 2, 128])
        ag = sb(top, "ag", [128, NB, 8])
        rw = sb(top, "rw", [128, NB, 8])
        sm4 = sb(top, "sm4", [128, NB, 8])
        cb = sb(top, "cb", [128, NB])
        R = {}

        z = pool.op(lambda e: e.memset(ident[:], 0.0))
        t_ident = pool.op(lambda e: e.affine_select(out=ident[:], in_=ident[:], compare_op=ALU.not_equal, fill=1.0,
                                                    base=0, pattern=[[-1, 128]], channel_multiplier=1), z)
        z1 = pool.op(lambda e: e.memset(mask_ts[:], 0.0))
        z2 = pool.op(lambda e: e.memset(mask_st[:], 0.0))
        t_m1 = pool.op(lambda e: e.affine_select(out=mask_ts[:], in_=mask_ts[:], compare_op=ALU.is_ge, fill=NEG,
                                                 base=0, pattern=[[-1, 128]], channel_multiplier=1), z1)
        t_m2 = pool.op(lambda e: e.affine_select(out=mask_st[:], in_=mask_st[:], compare_op=ALU.is_ge, fill=NEG,
                                                 base=0, pattern=[[1, 128]], channel_multiplier=-1), z2)
        t_identb = dve.op(lambda e: e.tensor_copy(identb[:], ident[:]), t_ident)
        t_consts = [t_ident, t_identb, t_m1, t_m2]

        col_at = {}
        n = 0
        for name, width in (("g1", 4), ("be1", 4), ("g2", 4), ("be2", 4), ("g3", 4), ("be3", 4), ("bq_s", 4),
                            ("bk_s", 4), ("bq_c", 4), ("bk_c", 4), ("bf1", 16), ("bt", 4), ("bv1", 4), ("bv_s", 4)):
            col_at[name] = n
            t_cols = sp.dma(lane("cols"), cols[:, n:n + width], A[name])
            n += width

        def col(name, k):
            return cols[:, col_at[name] + k:col_at[name] + k + 1]

        def fence():
            done = [q.last() for q in engines if q.n] + [(l[0], l[1]) for l in lanes.values()]
            for q in engines + [sp]:
                q.wait(done)

        def split_weight(src, raw, raw_free, hi, lo, ln):
            t = sp.dma(lane(ln), raw, src.rearrange("(k p) n -> p k n", p=128), raw_free)
            a = act.op(lambda e: e.activation(hi, raw, ACT.Copy), t)
            d = dve.op(lambda e: e.tensor_tensor(lo, raw, hi.bitcast(F32), ALU.subtract), t, a)
            return [a, d]

        def three(dst, lhs, rhs, start, stop, *tokens):
            pe.wait(*tokens)
            (lh, ll), (rh, rl) = lhs, rhs
            pe.op(lambda e: e.matmul(dst, lh, rh, start=start, stop=False), inc=False)
            pe.op(lambda e: e.matmul(dst, lh, rl, start=False, stop=False), inc=False)
            return pe.op(lambda e: e.matmul(dst, ll, rh, start=False, stop=stop), inc=stop)

        def layer_stats(xs, toks, sm):
            nt = len(xs)
            mv = sm[:, 64:64 + 2 * nt].rearrange("p (t a) -> p t a", a=2)
            st = sm[:, 0:6 * nt].rearrange("p (t a) -> p t a", a=6)
            ta = []
            for i, x in enumerate(xs):
                ta.append(dve.op(lambda e, i=i, x=x: e.bn_stats(st[:, i, :], x), toks[i]))
            tb = [dve.op(lambda e, i=i: e.bn_aggr(mv[:, i, :], st[:, i, :]), ta[i]) for i in range(nt)]
            v, r, u = (sm[:, 96 + 8 * j:96 + 8 * j + nt] for j in range(3))
            t = dve.op(lambda e: e.tensor_scalar(v, mv[:, :, 1], EPS, None, ALU.add), tb)
            t = act.op(lambda e: e.activation(u, v, ACT.Sqrt), t)
            t = dve.op(lambda e: e.reciprocal(r, u), t)
            t = dve.op(lambda e: e.tensor_tensor(u, r, r, ALU.mult), t)
            t = dve.op(lambda e: e.tensor_tensor(u, u, v, ALU.mult), t)
            t = dve.op(lambda e: e.tensor_scalar(u, u, -0.5, 1.5, ALU.mult, ALU.add), t)
            t = dve.op(lambda e: e.tensor_tensor(r, r, u, ALU.mult), t)
            return mv, r, t

        def normalise(xs, outs, toks, mv, r, t):
            got = []
            for i, (x, o) in enumerate(zip(xs, outs)):
                got.append(dve.op(lambda e, i=i, x=x, o=o: e.tensor_scalar(
                    o, x, mv[:, i, 0:1], r[:, i:i + 1], ALU.subtract, ALU.mult), t, toks[i]))
            return got

        def transposed(xs, toks, ring, ys, yfree, g, be, hi, lo, free):
            nt = len(xs)
            got, last = [], None
            for k in range(KT):
                b, ps, bfree = ring.take()
                for i, x in enumerate(xs):
                    t = pe.op(lambda e, i=i, x=x, ps=ps, k=k: e.transpose(
                        ps[:, 128 * i:128 * i + 128], x[:, 128 * k:128 * k + 128], ident[:]),
                        bfree, toks[i], t_ident, inc=i == nt - 1)
                last = t
                y = ys[k % 2][:, 0:128 * nt]
                t = act.op(lambda e, y=y, ps=ps, k=k: e.activation(
                    y, ps[:, 0:128 * nt], ACT.Identity, bias=col(be, k), scale=col(g, k)), t, yfree[k % 2], t_cols)
                ring.free[b] = [t]
                a = dve.op(lambda e, y=y, k=k: e.tensor_copy(hi[:, k, :], y), t, free)
                d = dve.op(lambda e, y=y, k=k: e.tensor_tensor(
                    lo[:, k, :], y, hi[:, k, :].bitcast(F32), ALU.subtract), a, t)
                yfree[k % 2] = [d]
                got.append(d)
                yield None
            yield got, last

        def phase0(ctx):
            wt = sb(ctx, "wt", [128, KT, C])
            wg = sb(ctx, "wg", [128, 8, C])
            wv = sb(ctx, "wv1", [128, KT, C])
            wh = sb(ctx, "wh", [128, KT, C], F32R)
            wl = sb(ctx, "wl", [128, KT, C], F32R)
            ct = sb(ctx, "ct4", [128, KT, NB, S])
            pl = sb(ctx, "pl", [128, KT, NB])
            vcol = sb(ctx, "vcol", [128, KT, NB])
            rows = sb(ctx, "rows", [NB, 2, C])
            orow = [sb(ctx, f"orow{i}", [NB, C]) for i in range(4)]
            ocb = sb(ctx, "ocb", [NB, 1])
            t_row = [sp.dma(lane("rows"), rows[0:NB, j, :], A[nm].partition_broadcast(NB))
                     for j, nm in enumerate(("bv1r", "bg"))][-1]
            t_ct = sp.dma(lane("ct"), ct[:], A["ctxT"].rearrange("(k p) (b s) -> p k b s", p=128, s=S))
            t_wv = sp.dma(lane("wv"), wv[:], A["Wv1"].rearrange("(k p) n -> p k n", p=128))
            t_wt = sp.dma(lane("wk"), wt[:], A["Wt"].rearrange("(k p) n -> p k n", p=128))
            t_wg = sp.dma(lane("bvc"), wg[:], A["Wg"].rearrange("(k p) n -> p k n", p=128))
            d0 = dve.op(lambda e: e.tensor_reduce(pl[:], ct[:], AX, ALU.add), t_ct)
            d1 = dve.op(lambda e: e.tensor_scalar(pl[:], pl[:], 1.0 / S, None, ALU.mult), d0)
            bt = cols[:, col_at["bt"]:col_at["bt"] + 4]
            ring = Banks(bank)

            def native(m, n, lhs, rhs, *tokens):
                b, ps, bfree = ring.take()
                for k in range(KT):
                    t = pe.op(lambda e, k=k, ps=ps: e.matmul(ps[0:m, 0:n], lhs(k), rhs(k), start=k == 0, stop=k == 3),
                              bfree, *tokens, inc=k == 3)
                return b, ps, t

            tv = []
            for m in range(4):
                b, ps, t = native(128, NB, lambda k, m=m: wv[:, k, 128 * m:128 * m + 128], lambda k: pl[:, k, :], t_wv, d1)
                d = dve.op(lambda e, m=m, ps=ps: e.tensor_scalar(vcol[:, m, :], ps[:, 0:NB], col("bv1", m), None, ALU.add), t, t_cols)
                ring.free[b] = [d]
                tv.append(d)
            b, ps, t = native(NB, C, lambda k: pl[:, k, :], lambda k: wv[:, k, :], t_wv, d1)
            d = dve.op(lambda e, ps=ps: e.tensor_tensor(orow[0][:], ps[0:NB, :], rows[:, 0, :], ALU.add), t, t_row)
            ring.free[b] = [d]
            sp.dma(lane("vp"), vp_d, orow[0][:], d)
            b, ps, t = native(NB, C, lambda k: vcol[:, k, :], lambda k: wt[:, k, :], tv, t_wt)
            a = act.op(lambda e, ps=ps: e.activation(orow[1][:], ps[0:NB, :], ACT.Copy), t)
            ring.free[b] = [a]
            sp.dma(lane("wvp"), wvp_d, orow[1][:], a)
            b, ps, t = native(NB, C, lambda k: vcol[:, k, :], lambda k: wg[:, 4 + k, :], tv, t_wg)
            a = act.op(lambda e, ps=ps: e.activation(orow[2][:], ps[0:NB, :], ACT.Copy), t)
            ring.free[b] = [a]
            sp.dma(lane("u"), u_d, orow[2][:], a)
            b, ps, t = native(NB, 1, lambda k: vcol[:, k, :], lambda k: bt[:, k:k + 1], tv, t_cols)
            a = act.op(lambda e, ps=ps: e.activation(ocb[:], ps[0:NB, 0:1], ACT.Copy), t)
            ring.free[b] = [a]
            sp.dma(lane("cb"), cb_d, ocb[:], a)
            b, ps, t = native(1, C, lambda k: bt[:, k:k + 1], lambda k: wg[:, k, :], t_cols, t_wg)
            d = dve.op(lambda e, ps=ps: e.tensor_tensor(orow[3][0:1, :], ps[0:1, :], rows[0:1, 1, :], ALU.add), t, t_row)
            ring.free[b] = [d]
            sp.dma(lane("gb"), gb_d, orow[3][0:1, :], d)
            for m in range(4):
                b, ps, t = native(128, C, lambda k, m=m: wt[:, k, 128 * m:128 * m + 128], lambda k: wg[:, k, :], t_wt, t_wg)
                a = act.op(lambda e, m=m, ps=ps: e.activation(wh[:, m, :], ps, ACT.Copy), t)
                d = dve.op(lambda e, m=m, ps=ps: e.tensor_tensor(wl[:, m, :], ps, wh[:, m, :].bitcast(F32), ALU.subtract), a)
                ring.free[b] = [a, d]
                sp.dma(lane("whl"), wh_d[128 * m:128 * m + 128, :], wh[:, m, :].bitcast(F32), a)
                sp.dma(lane("whl"), wl_d[128 * m:128 * m + 128, :], wl[:, m, :].bitcast(F32), d)
            fence()

        def phase1(ctx):
            W = {}
            for nm in ("q", "k", "v"):
                W[nm] = (sb(ctx, f"w{nm}h", [128, KT, C], F32R), sb(ctx, f"w{nm}l", [128, KT, C], F32R))
            er = sb(ctx, "er", [128, 8, 512])
            xr = sb(ctx, "xr", [128, 2, 512])
            ys = [sb(ctx, f"y{i}", [128, 256]) for i in range(2)]
            xh = sb(ctx, "xh", [128, KT, T], F32R)
            xl = sb(ctx, "xl", [128, KT, T], F32R)
            v = sb(ctx, "v", [128, 8, C])
            stage = [sb(ctx, f"stage{i}", [128, T], F32R) for i in range(4)]
            qs = [sb(ctx, f"qs{p}", [128, 4, T], F32R) for p in range(2)]
            ks = [sb(ctx, f"ks{p}", [128, 4, T], F32R) for p in range(2)]
            esum = [[sb(ctx, f"es{o}{i}", [128, 512]) for i in range(4)] for o in range(2)]
            ssb = sb(ctx, "ssb", [128, 512])
            sao = sb(ctx, "sao", [128, 512])
            mx = sb(ctx, "mx", [128, 160])
            ones = sb(ctx, "ones", [128, 32])

            t_ones = dve.op(lambda e: e.memset(ones[:], 1.0))
            t_mx0 = pool.op(lambda e: e.memset(mx[:], 0.0))
            oh = esum[0][0][96:128, 0:512].rearrange("p (i n) -> p i n", i=4)
            t = pool.op(lambda e: e.memset(oh, 0.0), t_mx0)
            t = pool.op(lambda e: e.affine_select(out=oh, in_=oh, compare_op=ALU.not_equal, fill=1.0, base=0,
                                                  pattern=[[-1, 4], [0, 128]], channel_multiplier=1), t)
            pool.wait(t)
            t_oh = [dve.op(lambda e, p=p, q=q: e.tensor_copy(
                ks[p][96:128, :, 128 * q:128 * q + 128], oh), t) for p in range(2) for q in range(8)]
            tw, rf = {}, [[], []]
            for j, nm in enumerate(("q", "k", "v")):
                tw[nm] = split_weight(A[f"W{nm}_s"], er[:, 4 * (j % 2):4 * (j % 2) + 4, :], rf[j % 2],
                                      W[nm][0][:], W[nm][1][:], f"raw{j % 2}")
                rf[j % 2] = tw[nm]

            ringB = Banks(bank[0:4])
            ringS = Banks(bank[4:6])
            ringO = Banks(bank[6:8])
            xfree = [[], []]
            yfree = [[], []]
            xhfree, vfree, stfree = [], [], []
            stack_free = [[], []]
            efree = [list(rf[i // 4]) for i in range(8)]
            esfree = [[[t_oh] for _ in range(4)] for _ in range(2)]
            ssfree, saofree = [], []
            mxfree = [t_mx0]
            state = {"e": 0, "o": 0, "fin": None}

            def gen_ln(b):
                got = []
                for qt in range(4):
                    toks = [sp.dma(lane(f"x{i}"), xr[:, i, :],
                                   x_d[b * T + qt * 256 + i * 128:b * T + qt * 256 + (i + 1) * 128, :], xfree[i])
                            for i in range(2)]
                    xs = [xr[:, i, :] for i in range(2)]
                    mv, r, t = layer_stats(xs, toks, small[:, 0, :])
                    yield 0.1
                    tn = normalise(xs, xs, toks, mv, r, t)
                    yield 0.1
                    ts = slice(256 * qt, 256 * qt + 256)
                    for step in transposed(xs, tn, ringB, ys, yfree, "g1", "be1", xh[:, :, ts], xl[:, :, ts], xhfree):
                        if step is None:
                            yield 1
                        else:
                            got.append(step[0])
                            for i in range(2):
                                xfree[i] = [step[1]]
                state["xn", b] = got

            def gen_proj(g):
                b, gg = divmod(g, 4)
                got = {}
                for c2 in range(2):
                    for w, nm in enumerate(("q", "k")):
                        bk, ps, bfree = ringB.take()
                        cs = slice(128 * gg, 128 * gg + 128)
                        ts = slice(512 * c2, 512 * c2 + 512)
                        for k in range(KT):
                            t = three(ps, (W[nm][0][:, k, cs], W[nm][1][:, k, cs]), (xh[:, k, ts], xl[:, k, ts]),
                                      k == 0, k == KT - 1, bfree, tw[nm], state["xn", b][2 * c2][k],
                                      state["xn", b][2 * c2 + 1][k])
                            yield 3
                        hi, lo = stage[2 * w][:, ts], stage[2 * w + 1][:, ts]
                        bias = col(f"b{nm}_s", gg)
                        a = act.op(lambda e, hi=hi, ps=ps, bias=bias: e.activation(
                            hi, ps, ACT.Identity, bias=bias, scale=1.0), t, stfree, t_cols)
                        d = dve.op(lambda e, hi=hi, lo=lo, ps=ps, bias=bias: e.scalar_tensor_tensor(
                            lo, ps, bias, hi.bitcast(F32), ALU.add, ALU.subtract), a, stfree)
                        ringB.free[bk] = [a, d]
                        got[w, c2] = [a, d]
                state["stage", g] = got
                if gg == 3:
                    xhfree[:] = [t]

            def stack(g):
                par = g % 2
                tl = {}
                for c2 in range(2):
                    ts = slice(512 * c2, 512 * c2 + 512)
                    for w, order in ((0, (0, 1, 0)), (1, (0, 0, 1))):
                        for r, part in enumerate(order):
                            tl[w, c2] = sp.dma(lane(f"stk{par}{w}{c2}"),
                                               (qs, ks)[w][par][32 * r:32 * r + 32, :, ts].bitcast(F32),
                                               stage[2 * w + part][:, ts].bitcast(F32),
                                               state["stage", g][w, c2], stack_free[par])
                stfree[:] = list(tl.values())
                state["stack", g] = tl

            def gen_max(g):
                par = g % 2
                tl = state["stack", g]
                tm = []
                for ti in range(8):
                    wd = 128 * (ti + 1)
                    per = 4 if ti < 2 else 2 if ti < 4 else 1
                    need = [tl[0, 0], tl[1, 0]] + ([tl[0, 1], tl[1, 1]] if ti >= 4 else [])
                    for h0 in range(0, 4, per):
                        b0, _, f0 = ringB.take()
                        b1, _, f1 = ringB.take()
                        pair = psum[:, b0:b0 + 2, :].rearrange("p a n -> p (a n)")
                        stride = 128 if ti == 0 else 256 if ti == 1 else 512
                        for u in range(per):
                            i = h0 + u
                            q = qs[par][0:96, i, 128 * ti:128 * ti + 128]
                            for c0 in range(0, wd, 512):
                                w = min(512, wd - c0)
                                at = u * stride + c0
                                diag = c0 + w == wd
                                pe.op(lambda e, q=q, i=i, at=at, w=w, c0=c0, pair=pair, diag=diag: e.matmul(
                                    pair[:, at:at + w], q, ks[par][0:96, i, c0:c0 + w], start=True, stop=not diag),
                                    need, f0, f1, inc=False)
                                if diag:
                                    t = pe.op(lambda e, at=at, w=w, pair=pair: e.matmul(
                                        pair[:, at + w - 128:at + w], identb[:], mask_ts[:], start=False, stop=True),
                                        t_consts, inc=u == per - 1)
                        src = pair[:, 0:per * stride].rearrange("p (u n) -> p u n", u=per)[:, :, 0:wd] if per > 1 else pair[:, 0:wd]
                        at = 96 + 4 * ti + h0
                        d = dve.op(lambda e, at=at, per=per, src=src: e.tensor_reduce(
                            mx[:, at:at + per], src, AX, ALU.max, negate=True), t, mxfree)
                        ringB.free[b0] = [d]
                        ringB.free[b1] = [d]
                        tm.append(d)
                        yield per * (wd + 128) / 512
                b0, _, f0 = ringB.take()
                b1, _, f1 = ringB.take()
                for ti in range(8):
                    t = pe.op(lambda e, ti=ti, b0=b0: e.transpose(
                        bank[b0 + ti // 4][:, 128 * (ti % 4):128 * (ti % 4) + 128], mx[:, 4 * ti:4 * ti + 128], ident[:]),
                        tm, f0, f1, t_ident, inc=ti == 7)
                mxfree[:] = [t]
                pair = psum[96:128, b0:b0 + 2, :].rearrange("p a n -> p (a n)")
                tq = [act.op(lambda e, i=i, pair=pair: e.activation(qs[par][96:128, i, :], pair, ACT.Copy),
                             t, stack_free[par]) for i in range(4)]
                ringB.free[b0] = ringB.free[b1] = [tq[3]]
                state["max", g] = tq
                yield 4

            def gen_v(b):
                got = []
                for st in range(8):
                    bk, ps, bfree = ringS.take()
                    for k in range(KT):
                        ss = slice(128 * st, 128 * st + 128)
                        t = three(ps, (xh[:, k, ss], xl[:, k, ss]), (W["v"][0][:, k, :], W["v"][1][:, k, :]),
                                  k == 0, k == KT - 1, bfree, tw["v"], state["xn", b][st // 2][k])
                        yield 3
                    d = act.op(lambda e, ps=ps, st=st: e.activation(v[:, st, :], ps, ACT.Copy), t, vfree)
                    ringS.free[bk] = [d]
                    got.append(d)
                    if st == 3:
                        finish()
                state["v", b] = got

            def finish():
                if state["fin"] is None:
                    return
                g, c2, o, ob, po, tsum, tpv = state["fin"]
                state["fin"] = None
                b, gg = divmod(g, 4)
                sbk, ps, sfree = ringS.take()
                for i in range(4):
                    t = pe.op(lambda e, i=i, ps=ps: e.matmul(ps[32 * i:32 * i + 32, :], ones[:], esum[o][i][:],
                                                             start=True, stop=True), tsum[i], sfree, t_ones)
                    esfree[o][i] = [t]
                a = dve.op(lambda e, ps=ps: e.reciprocal(ssb[:], ps), t, ssfree)
                ringS.free[sbk] = [a]
                d = dve.op(lambda e, po=po: e.tensor_tensor(sao[:], po, ssb[:], ALU.mult), a, tpv, saofree)
                ssfree[:] = [d]
                ringO.free[ob] = [d]
                t0 = b * T + c2 * 512
                saofree[:] = [sp.dma(lane("sa"), sa_d[128 * gg:128 * gg + 128, t0:t0 + 512], sao[:], d)]

            def gen_a(g):
                b, gg = divmod(g, 4)
                par = g % 2
                if gg == 0:
                    yield from gen_v(b)
                tv = state["v", b]
                tl, tq = state["stack", g], state["max", g]
                for c2 in range(2):
                    o = state["o"] % 2
                    state["o"] += 1
                    ob, po, ofree = ringO.take()
                    nj = 4 * c2 + 4
                    tsum = [None] * 4
                    pending = []

                    def products(i, jj, off, dst, slot, x, po, nj, o):
                        t = pe.op(lambda e: e.matmul(
                            po[32 * i:32 * i + 32, off:512], v[:, jj, 128 * gg + 32 * i:128 * gg + 32 * i + 32],
                            dst[:, off:512], start=jj == 0, stop=jj == nj - 1), x, tv[jj], ofree)
                        if jj == 0:
                            tsum[i] = t
                        else:
                            tsum[i] = pool.op(lambda e: e.tensor_tensor(
                                esum[o][i][:, off:512], esum[o][i][:, off:512], dst[:, off:512], ALU.add), tsum[i], x)
                            efree[slot] = [tsum[i], t]
                        return t

                    for j in range(nj):
                        off = max(0, 128 * (j - 4 * c2))
                        for i in range(4):
                            sbk, ps, sfree = ringS.take()
                            t = pe.op(lambda e, i=i, j=j, ps=ps, off=off, c2=c2: e.matmul(
                                ps[:, off:512], ks[par][:, i, 128 * j:128 * j + 128],
                                qs[par][:, i, 512 * c2 + off:512 * c2 + 512], start=True, stop=j < 4 * c2),
                                sfree, [tl[0, c2], tl[1, 0]] + ([tl[1, 1]] if j >= 4 else []), tq[i], t_oh, inc=j < 4 * c2)
                            if j >= 4 * c2:
                                t = pe.op(lambda e, ps=ps, off=off: e.matmul(
                                    ps[:, off:off + 128], identb[:], mask_st[:], start=False, stop=True), t_consts)
                            if j == 0:
                                dst, free, slot = esum[o][i], esfree[o][i], None
                            else:
                                slot = state["e"] % 8
                                state["e"] += 1
                                dst, free = er[:, slot, :], efree[slot]
                            x = act.op(lambda e, dst=dst, ps=ps, off=off: e.activation(
                                dst[:, off:512], ps[:, off:512], ACT.Exp, scale=SCALE), t, free)
                            ringS.free[sbk] = [x]
                            pending.append((i, j, off, dst, slot, x))
                            yield 1.2 * (512 - off) / 512
                            if i == 3 and len(pending) > 4:
                                for _ in range(4):
                                    tpv = products(*pending.pop(0), po, nj, o)
                                yield 4 * (512 - off) / 512
                        if j == 2:
                            finish()
                    while pending:
                        tpv = products(*pending.pop(0), po, nj, o)
                    yield 1
                    state["fin"] = (g, c2, o, ob, po, tsum, tpv)
                stack_free[par][:] = [t]
                if gg == 3:
                    vfree[:] = [tpv]

            def chain(*gens):
                for x in gens:
                    yield from x

            for x in chain(gen_ln(0), gen_proj(0)):
                pass
            stack(0)
            for x in chain(gen_proj(1), gen_max(0)):
                pass
            for g in range(16):
                todo, total = [], 0
                if g < 15:
                    stack(g + 1)
                if g + 2 < 16:
                    if (g + 2) % 4 == 0:
                        todo.append(gen_ln((g + 2) // 4))
                        total += 17
                    todo.append(gen_proj(g + 2))
                    total += 48
                if g < 15:
                    todo.append(gen_max(g + 1))
                    total += 49
                merge(gen_a(g), chain(*todo), 88 + (96 if g % 4 == 0 else 0), max(total, 1))
            finish()
            fence()

        def phase2(ctx):
            W = {}
            for nm in ("W1", "Wq_c", "W2"):
                W[nm] = (sb(ctx, f"{nm}h", [128, KT, C], F32R), sb(ctx, f"{nm}l", [128, KT, C], F32R))
            kbh = sb(ctx, "kbh", [128, NB, 4, 256], F32R)
            kbl = sb(ctx, "kbl", [128, NB, 4, 256], F32R)
            vb = sb(ctx, "vb", [128, NB, C])
            b1b = sb(ctx, "b1b", [128, C])
            b2b = sb(ctx, "b2b", [128, C])
            xt = [sb(ctx, f"xt{p}", [128, 4, C]) for p in range(3)]
            sx = sb(ctx, "sx", [128, 4, C])
            ah = sb(ctx, "ah", [128, KT, 512], F32R)
            al = sb(ctx, "al", [128, KT, 512], F32R)
            qh = [sb(ctx, f"qh{p}", [128, 4, 512], F32R) for p in range(2)]
            ql = [sb(ctx, f"ql{p}", [128, 4, 512], F32R) for p in range(2)]
            pp = [sb(ctx, f"pp{p}", [128, 16, S]) for p in range(2)]
            pT = [sb(ctx, f"pT{p}", [128, 8, 128]) for p in range(2)]
            ch = [sb(ctx, f"ch{p}", [128, 4, 128], F32R) for p in range(2)]
            cl = [sb(ctx, f"cl{p}", [128, 4, 128], F32R) for p in range(2)]
            ys = [sb(ctx, f"y2{i}", [128, 512]) for i in range(2)]

            tw, rfree = {}, [[], []]
            raws = [xt[1][:], xt[2][:]]

            def weight(j, nm):
                tw[nm] = split_weight(A[nm], raws[j], rfree[j], W[nm][0][:], W[nm][1][:], f"raw{j}")
                rfree[j] = tw[nm]

            weight(0, "W1")
            weight(1, "Wq_c")
            t_b1 = sp.dma(lane("b1"), b1b[:], A["b1"].partition_broadcast(128))
            t_b2 = sp.dma(lane("b2"), b2b[:], A["b2"].partition_broadcast(128))
            nm_ = [sb(ctx, f"nm{p}", [128, 16]) for p in range(2)]
            sm_ = [sb(ctx, f"sm{p}", [128, 16]) for p in range(2)]

            ringI = Banks(bank[0:3])
            xfree = [[[] for _ in range(4)] for _ in range(3)]
            F = {"s": [], "a": [], "y": [[], []], "q": [[], []]}
            Q, X = {}, {}

            def chunk(c):
                p, b = c % 3, c // 2
                t0 = 512 * c
                xs = [xt[p][:, i, :] for i in range(4)]
                ts_ = sp.dma(lane("cs"), sx[:], sa_d[:, t0:t0 + 512].rearrange("(k p) n -> p k n", p=128), F["s"])
                tx = [sp.dma(lane(f"cx{p}{i}"), xs[i], x_d[t0 + 128 * i:t0 + 128 * i + 128, :], xfree[p][i]) for i in range(4)]
                yield 0.1
                tsp = []
                for k in range(KT):
                    a = act.op(lambda e, k=k: e.activation(ah[:, k, :], sx[:, k, :], ACT.Identity, bias=col("bv_s", k),
                                                           scale=1.0), ts_, F["a"])
                    tsp.append(dve.op(lambda e, k=k: e.scalar_tensor_tensor(
                        al[:, k, :], sx[:, k, :], col("bv_s", k), ah[:, k, :].bitcast(F32), ALU.add, ALU.subtract), a))
                tb = [pool.op(lambda e, i=i: e.tensor_tensor(xs[i], xs[i], b1b[:], ALU.add), tx[i], t_b1) for i in range(4)]
                yield 0.1
                t1 = []
                for i in range(4):
                    bk, ps, bfree = ringI.take()
                    r = slice(128 * i, 128 * i + 128)
                    for k in range(KT):
                        t = three(ps, (ah[:, k, r], al[:, k, r]), (W["W1"][0][:, k, :], W["W1"][1][:, k, :]),
                                  k == 0, k == 3, bfree, tsp[k], tw["W1"])
                        yield 3
                    d = dve.op(lambda e, i=i, ps=ps: e.tensor_tensor(xs[i], ps, xs[i], ALU.add), t, tb[i])
                    ringI.free[bk] = [d]
                    t1.append(d)
                ta = t
                mv, r_, tr = layer_stats(xs, t1, small[:, 0, :])
                yield 0.1
                xn = [sx[:, i, :] for i in range(4)]
                tn = normalise(xs, xn, t1, mv, r_, tr)
                X[c] = [pool.op(lambda e, i=i: e.tensor_tensor(xs[i], xs[i], b2b[:], ALU.add), tn[i], t_b2) for i in range(4)]
                yield 0.1
                for step in transposed(xn, tn, ringI, ys, F["y"], "g2", "be2", ah, al, [ta]):
                    if step is None:
                        yield 2
                    else:
                        txn, tl = step
                F["s"] = [tl]
                tq = []
                qp = c % 2
                for m in range(4):
                    bk, ps, bfree = ringI.take()
                    for k in range(KT):
                        t = three(ps, tuple(W["Wq_c"][j][:, k, 128 * m:128 * m + 128] for j in range(2)),
                                  (ah[:, k, :], al[:, k, :]), k == 0, k == 3, bfree, txn[k], tw["Wq_c"])
                        yield 3
                    a = act.op(lambda e, m=m, ps=ps: e.activation(qh[qp][:, m, :], ps, ACT.Identity, bias=col("bq_c", m),
                                                                  scale=1.0), t, F["q"][qp])
                    d = dve.op(lambda e, m=m, ps=ps: e.scalar_tensor_tensor(
                        ql[qp][:, m, :], ps, col("bq_c", m), qh[qp][:, m, :].bitcast(F32), ALU.add, ALU.subtract),
                        a, F["q"][qp])
                    ringI.free[bk] = [a, d]
                    tq.append(d)
                F["a"] = [t]
                Q[c] = tq

            ringP = Banks(bank[3:5])
            ringT = Banks(bank[5:8])
            wkv = [sb(ctx, "wkv", [128, KT, C])]
            ct = sb(ctx, "ctc", [128, KT, 256])
            bvc = pT[0][:].rearrange("p a n -> p (a n)")[:, 0:512]
            t_ct = sp.dma(lane("ct"), ct[:], A["ctxT"].rearrange("(k p) n -> p k n", p=128))
            t_wk = sp.dma(lane("wk"), wkv[0][:], A["Wk_c"].rearrange("(k p) n -> p k n", p=128))
            t_bvc = sp.dma(lane("bvc"), bvc, A["bv_c"].partition_broadcast(128))
            tz = [pool.op(lambda e, q=q: e.memset(q, 0.0)) for q in (kbh[:].bitcast(F32), kbl[:].bitcast(F32), vb[:])]
            cd = [pp[0][:].rearrange("p h s -> p (h s)"), pp[1][:].rearrange("p h s -> p (h s)")]
            td = [dve.op(lambda e, k=k, j=j: e.tensor_copy(
                cd[k // 2][:, 512 * (k % 2):512 * (k % 2) + 512].rearrange("p (b j s) -> p b j s", j=2, s=S)[:, :, j, :],
                ct[:, k, :].rearrange("p (b s) -> p b s", s=S)), t_ct) for k in range(KT) for j in range(2)]
            t_kv = []

            def context():
                for m in range(4):
                    b, ps, bfree = ringT.take()
                    for k in range(KT):
                        t = pe.op(lambda e, m=m, k=k, ps=ps: e.matmul(
                            ps[:, 0:256], wkv[0][:, k, 128 * m:128 * m + 128], ct[:, k, :], start=k == 0, stop=k == 3),
                            t_ct, t_wk, bfree, inc=k == 3)
                    for i in range(4):
                        r = slice(32 * i, 32 * i + 32)
                        src = ps[r, 0:256].rearrange("p (b s) -> p b s", s=S)
                        dh, dl = (q[r, :, m, 64 * i:64 * i + 64] for q in (kbh, kbl))
                        bias = cols[r, col_at["bk_c"] + m:col_at["bk_c"] + m + 1]
                        a = act.op(lambda e, dh=dh, src=src, bias=bias: e.activation(
                            dh, src, ACT.Identity, bias=bias, scale=1.0), t, tz, t_cols)
                        t_kv.append(dve.op(lambda e, dh=dh, dl=dl, src=src, bias=bias: e.scalar_tensor_tensor(
                            dl, src, bias, dh.bitcast(F32), ALU.add, ALU.subtract), a, tz))
                    ringT.free[b] = [a, t_kv[-1]]
                    yield 8
                t_wv = sp.dma(lane("wk"), wkv[0][:], A["Wv_c"].rearrange("(k p) n -> p k n", p=128), t)
                weight(0, "W2")
                for b in range(NB):
                    bk, ps, bfree = ringT.take()
                    for k in range(KT):
                        t = pe.op(lambda e, b=b, k=k, ps=ps: e.matmul(
                            ps, cd[k // 2][:, 512 * (k % 2) + 128 * b:512 * (k % 2) + 128 * b + 128], wkv[0][:, k, :],
                            start=k == 0, stop=k == 3), td, t_wv, bfree, inc=k == 3)
                    for j in range(2):
                        r = slice(64 * j, 64 * j + 64)
                        o, i0, i1 = (q.rearrange("p (h j d) -> p h j d", j=2, d=DH)[:, :, j, :]
                                     for q in (vb[r, b, :], ps[r, :], bvc[r, :]))
                        t_kv.append(dve.op(lambda e, o=o, i0=i0, i1=i1: e.tensor_tensor(o, i0, i1, ALU.add), t, tz, t_bvc))
                    ringT.free[bk] = [t_kv[-1]]
                    yield 16
                for i in range(2):
                    ppfree[i], pTfree[i] = [t], [t_kv[-1]]
                for i in range(4):
                    xfree[1][i] = rfree[0]
                    xfree[2][i] = rfree[1]

            ppfree, pTfree, cfree = [[], []], [[], []], [[], []]
            S_, P_, V_ = {}, {}, {}

            def scores(n):
                c, i = divmod(n, 4)
                b, qp, p = c // 2, c % 2, n % 2
                r = slice(128 * i, 128 * i + 128)
                b0, _, f0 = ringP.take()
                b1, _, f1 = ringP.take()
                for m in range(4):
                    ps = ringP.aps[b0 + m // 2][:, 256 * (m % 2):256 * (m % 2) + 256]
                    t = three(ps, (qh[qp][:, m, r], ql[qp][:, m, r]), (kbh[:, b, m, :], kbl[:, b, m, :]),
                              True, True, f0, f1, Q[c][m], t_kv)
                    yield 1.5
                if i == 3:
                    F["q"][qp] = [t]
                sc = psum[:, 3:5, :].rearrange("p a (h s) -> p (a h) s", s=S)
                t = dve.op(lambda e: e.tensor_reduce(nm_[p][:], sc, AX, ALU.max, negate=True), t)
                t = dve.op(lambda e: e.tensor_tensor(pp[p][:], sc, nm_[p][:].unsqueeze(2).broadcast_to((128, 16, S)),
                                                     ALU.add), t, ppfree[p])
                ringP.free[b0] = ringP.free[b1] = [t]
                S_[n] = act.op(lambda e: e.activation(pp[p][:], pp[p][:], ACT.Exp, scale=SCALE), t)

            def weights(n):
                p = n % 2
                t4 = dve.op(lambda e: e.tensor_reduce(sm_[p][:], pp[p][:], AX, ALU.add), S_[n])
                t5 = dve.op(lambda e: e.reciprocal(nm_[p][:], sm_[p][:]), t4)
                P_[n] = pool.op(lambda e: e.tensor_tensor(pp[p][:], pp[p][:], nm_[p][:].unsqueeze(2).broadcast_to((128, 16, S)),
                                                          ALU.mult), t5)

            def turn(n):
                p = n % 2
                V_[n] = []
                for hf in range(2):
                    bk, ps, bfree = ringT.take()
                    for u in range(4):
                        pr = 4 * hf + u
                        t = pe.op(lambda e, pr=pr, u=u, ps=ps: e.transpose(
                            ps[:, 128 * u:128 * u + 128], pp[p][:, 2 * pr:2 * pr + 2, :].rearrange("p h s -> p (h s)"),
                            ident[:]), P_[n], bfree, inc=u == 3)
                    a = act.op(lambda e, hf=hf, ps=ps: e.activation(
                        pT[p][:, 4 * hf:4 * hf + 4, :], ps.rearrange("p (u t) -> p u t", u=4), ACT.Copy), t, pTfree[p])
                    ringT.free[bk] = [a]
                    V_[n].append(a)
                    yield 2
                ppfree[p] = [t]

            C_ = {}

            def values(n):
                c, p = n // 4, n % 2
                b = c // 2
                bk, ps, bfree = ringT.take()
                for pr in range(8):
                    t = pe.op(lambda e, pr=pr, ps=ps: e.matmul(
                        ps[64 * (pr % 2):64 * (pr % 2) + 64, 128 * (pr // 2):128 * (pr // 2) + 128],
                        vb[:, b, 64 * pr:64 * pr + 64], pT[p][:, pr, :], start=True, stop=True),
                        V_[n], bfree, t_kv, inc=pr == 7)
                pTfree[p] = [t]
                pv = ps.rearrange("p (k t) -> p k t", k=4)
                a = act.op(lambda e, pv=pv: e.activation(ch[p][:], pv, ACT.Copy), t, cfree[p])
                C_[n] = dve.op(lambda e, pv=pv: e.tensor_tensor(cl[p][:], pv, ch[p][:].bitcast(F32), ALU.subtract), a, cfree[p])
                ringT.free[bk] = [a, C_[n]]
                yield 5

            def project(n):
                c, i = divmod(n, 4)
                p, px = n % 2, c % 3
                x = xt[px][:, i, :]
                bk, ps, bfree = ringT.take()
                for k in range(KT):
                    t = three(ps, (ch[p][:, k, :], cl[p][:, k, :]), (W["W2"][0][:, k, :], W["W2"][1][:, k, :]),
                              k == 0, k == 3, bfree, C_[n], tw["W2"])
                    yield 3
                cfree[p] = [t]
                d = dve.op(lambda e, ps=ps: e.tensor_tensor(x, ps, x, ALU.add), t, X[c][i])
                ringT.free[bk] = [d]
                xfree[px][i] = [sp.dma(lane(f"sx{px}{i}"), x2_d[128 * n:128 * n + 128, :], x, d)]

            def tiles(ns):
                for n in ns:
                    if n < 32:
                        yield from scores(n)
                    if 0 <= n - 3 < 32:
                        yield from project(n - 3)
                    if 0 <= n - 1 < 32:
                        yield from turn(n - 1)
                    if 0 <= n - 2 < 32:
                        yield from values(n - 2)
                    if n < 32:
                        weights(n)
                    yield 0.1

            merge(chunk(0), context(), 115, 96)
            for c in range(8):
                merge(tiles(range(4 * c, 4 * c + 4)), chunk(c + 1) if c < 7 else iter(()), 110, 115)
            for _ in tiles(range(32, 35)):
                pass
            fence()

        def phase3(ctx):
            f1h, f1l = (sb(ctx, f"f1{j}", [128, KT, 2048], F32R) for j in "hl")
            f2h, f2l = (sb(ctx, f"f2{j}", [128, 16, C], F32R) for j in "hl")
            xt = [sb(ctx, f"fx{p}", [128, 2, C]) for p in range(2)]
            xn_ = [sb(ctx, f"fn{p}", [128, 2, C]) for p in range(2)]
            ah = [sb(ctx, f"fah{p}", [128, KT, 256], F32R) for p in range(2)]
            al = [sb(ctx, f"fal{p}", [128, KT, 256], F32R) for p in range(2)]
            hh = [[sb(ctx, f"hh{p}{q}", [128, 4, 256], F32R) for q in range(2)] for p in range(2)]
            hl = [[sb(ctx, f"hl{p}{q}", [128, 4, 256], F32R) for q in range(2)] for p in range(2)]
            yb = [sb(ctx, f"fy{p}", [128, 512]) for p in range(2)]
            y2 = [[yb[p][:, 256 * i:256 * i + 256] for i in range(2)] for p in range(2)]
            bfb = sb(ctx, "bfb", [128, C])
            t_bf = sp.dma(lane("bf"), bfb[:], A["bf2"].partition_broadcast(128))
            raw = [xt[0][:].rearrange("p a n -> p (a n)"), xt[1][:].rearrange("p a n -> p (a n)"),
                   xn_[0][:].rearrange("p a n -> p (a n)"), xn_[1][:].rearrange("p a n -> p (a n)")]
            rf = [[] for _ in raw]
            tw1, tw2 = [], []
            n = 0
            for kind in range(2):
                for u in range(8):
                    j = n % 4
                    n += 1
                    if kind == 0:
                        k, hf = divmod(u, 2)
                        src = A["Wf1"][128 * k:128 * k + 128, 1024 * hf:1024 * hf + 1024]
                        rr = raw[j]
                        hi, lo = (q[:, k, 1024 * hf:1024 * hf + 1024] for q in (f1h, f1l))
                    else:
                        src = A["Wf2"][256 * u:256 * u + 256, :].rearrange("(k p) n -> p k n", p=128)
                        rr = raw[j].rearrange("p (k n) -> p k n", k=2)
                        hi, lo = (q[:, 2 * u:2 * u + 2, :] for q in (f2h, f2l))
                    t = sp.dma(lane(f"fr{j}"), rr, src, rf[j])
                    a = act.op(lambda e, hi=hi, rr=rr: e.activation(hi, rr, ACT.Copy), t)
                    d = dve.op(lambda e, hi=hi, lo=lo, rr=rr: e.tensor_tensor(lo, rr, hi.bitcast(F32), ALU.subtract), t, a)
                    rf[j] = [a, d]
                    (tw1, tw2)[kind].append(d)
            wvb = [sb(ctx, f"wvb{i}", [128, C]) for i in range(2)]
            jk = sb(ctx, "jk", [128, C])
            t_wvb = {b: sp.dma(lane(f"wvb{b}"), wvb[b][:], wvp_d[b, :].partition_broadcast(128)) for b in range(2)}
            t_cb = sp.dma(lane("cbb"), cb[:], cb_d.rearrange("b a -> (b a)").partition_broadcast(128))
            agt = {}

            def route(b):
                d = dve.op(lambda e: e.tensor_scalar(ag[:, b, :], ag[:, b, :], cb[:, b:b + 1], 2.0, ALU.add, ALU.mult),
                           agt[b], t_cb)
                d = dve.op(lambda e: e.tensor_reduce(sm4[:, b, 0:1], ag[:, b, :], AX, ALU.max), d)
                p = pool.op(lambda e: e.partition_all_reduce(sm4[:, b, 1:2], sm4[:, b, 0:1], 128, bass.bass_isa.ReduceOp.max), d)
                d = dve.op(lambda e: e.tensor_scalar(sm4[:, b, 2:3], sm4[:, b, 1:2], -1.0, None, ALU.mult), p)
                a = act.op(lambda e: e.activation(rw[:, b, :], ag[:, b, :], ACT.Exp, bias=sm4[:, b, 2:3], scale=1.0,
                                                  accum_out=sm4[:, b, 3:4]), d)
                p = pool.op(lambda e: e.partition_all_reduce(sm4[:, b, 4:5], sm4[:, b, 3:4], 128, bass.bass_isa.ReduceOp.add), a)
                d = dve.op(lambda e: e.reciprocal(sm4[:, b, 5:6], sm4[:, b, 4:5]), p)
                R["rw", b] = dve.op(lambda e: e.tensor_scalar(rw[:, b, :], rw[:, b, :], sm4[:, b, 5:6], None, ALU.mult), d, a)

            accs = [Banks(bank[0:2]), Banks(bank[4:6])]
            rings = [Banks(bank[2:4]), Banks(bank[6:8])]
            F = [{"x": [rf[p], rf[p]], "n": [rf[2 + p]], "a": [], "h": [[], []], "y": [[], []], "yb": []} for p in range(2)]

            def chunk3(c):
                p = c % 2
                f, ring = F[p], rings[p]
                t0 = 256 * c
                xs = [xt[p][:, i, :] for i in range(2)]
                xn = [xn_[p][:, i, :] for i in range(2)]
                tx = [sp.dma(lane(f"fx{p}{i}"), xs[i], x2_d[t0 + 128 * i:t0 + 128 * i + 128, :], f["x"][i]) for i in range(2)]
                yield
                mv, r_, tr = layer_stats(xs, tx, small[:, p, :])
                yield
                dve.wait(f["n"])
                tn = normalise(xs, xn, tx, mv, r_, tr)
                tb = [pool.op(lambda e, i=i: e.tensor_tensor(xs[i], xs[i], bfb[:], ALU.add), tn[i], t_bf) for i in range(2)]
                yield
                for step in transposed(xn, tn, ring, y2[p], f["y"], "g3", "be3", ah[p], al[p], f["a"]):
                    if step is None:
                        yield
                    else:
                        txn, tl = step
                f["n"] = [tl]
                f["yb"] = f["y"][0] + f["y"][1]
                acc = [accs[p].take() for _ in range(2)]
                prev = None
                for qd in range(5):
                    if qd < 4:
                        th = []
                        hb = qd % 2
                        for m2 in range(2):
                            bk, ps, bfree = ring.take()
                            ty = []
                            for u in range(2):
                                m = 4 * qd + 2 * m2 + u
                                for k in range(KT):
                                    t = three(ps[:, 256 * u:256 * u + 256],
                                              tuple(q[:, k, 128 * m:128 * m + 128] for q in (f1h, f1l)),
                                              (ah[p][:, k, :], al[p][:, k, :]), k == 0, k == 3, bfree, txn[k],
                                              tw1[2 * k + m // 8])
                            for u in range(2):
                                m = 4 * qd + 2 * m2 + u
                                ty.append(act.op(lambda e, u=u, m=m, ps=ps: e.activation(
                                    yb[p][:, 256 * u:256 * u + 256], ps[:, 256 * u:256 * u + 256], ACT.Relu,
                                    bias=col("bf1", m), scale=1.0), t, f["yb"]))
                            ring.free[bk] = [ty[-1]]
                            yv = yb[p][:].rearrange("p (m t) -> p m t", m=2)
                            hi, lo = (q[p][hb][:, 2 * m2:2 * m2 + 2, :] for q in (hh, hl))
                            a = dve.op(lambda e, hi=hi, yv=yv: e.tensor_copy(hi, yv), ty, f["h"][hb])
                            d = dve.op(lambda e, hi=hi, lo=lo, yv=yv: e.tensor_tensor(lo, yv, hi.bitcast(F32), ALU.subtract), a)
                            f["yb"] = [d]
                            th.append(d)
                            yield
                        if qd == 3:
                            f["a"] = [t]
                        cur = (qd, hb, th)
                    else:
                        cur = None
                    if prev:
                        q0, hb, th = prev
                        for i in range(2):
                            ab, ps, afree = acc[i]
                            for m in range(4):
                                r = slice(128 * i, 128 * i + 128)
                                t = three(ps, (hh[p][hb][:, m, r], hl[p][hb][:, m, r]),
                                          (f2h[:, 4 * q0 + m, :], f2l[:, 4 * q0 + m, :]), q0 == 0 and m == 0, q0 == 3 and m == 3,
                                          afree, th[m // 2], tw2[2 * q0 + m // 2])
                            if q0 < 3 and i == 1:
                                pe.items[-1] = (pe.items[-1][0], pe.sem, 1)
                                pe.n += 1
                                t = pe.last()
                            if q0 == 3:
                                d = dve.op(lambda e, i=i, ps=ps: e.tensor_tensor(xs[i], ps, xs[i], ALU.add), t, tb[i])
                                accs[p].free[ab] = [d]
                                b, tt = divmod(2 * c + i, 8)
                                g = dve.op(lambda e, i=i, b=b, tt=tt: e.tensor_tensor_reduce(
                                    out=jk[:], in0=xs[i], in1=wvb[b % 2][:], scale=1.0, scalar=0.0, op0=ALU.mult,
                                    op1=ALU.add, accum_out=ag[:, b, tt:tt + 1]), d, t_wvb[b], agt.get(b))
                                agt[b] = g
                                if tt == 7:
                                    if b + 2 < NB:
                                        t_wvb[b + 2] = sp.dma(lane(f"wvb{b + 2}"), wvb[b % 2][:],
                                                              wvp_d[b + 2, :].partition_broadcast(128), g)
                                    route(b)
                                f["x"][i] = [sp.dma(lane(f"fs{p}{i}"), x3_d[t0 + 128 * i:t0 + 128 * i + 128, :], xs[i], d), g]
                            yield
                        f["h"][hb] = [t]
                    prev = cur
                f["y"] = [list(f["yb"]), list(f["yb"])]

            window([chunk3(c) for c in range(16)], 8)
            fence()

        def phase4(ctx):
            wh = sb(ctx, "wh4", [128, KT, C], F32R)
            wl = sb(ctx, "wl4", [128, KT, C], F32R)
            vpb = sb(ctx, "vpb", [128, NB, C])
            ub = sb(ctx, "ub", [128, NB, C])
            gb = sb(ctx, "gb", [128, C])
            rows = sb(ctx, "rows4", [128, 2, C])
            NX, NG = 16, 16
            x3 = [sb(ctx, f"x3{i}", [128, C]) for i in range(NX)]
            th_ = [sb(ctx, f"th{p}", [128, KT, 128], F32R) for p in range(4)]
            tl_ = [sb(ctx, f"tl{p}", [128, KT, 128], F32R) for p in range(4)]
            gt = [sb(ctx, f"gt{p}", [128, C]) for p in range(NG)]

            x3free = [[] for _ in range(NX)]
            X = {}

            def load(n):
                X[n] = sp.dma(lane(f"g{n % NX}"), x3[n % NX][:], x3_d[128 * n:128 * n + 128, :], x3free[n % NX])

            for n in range(4):
                load(n)
            t_w = [sp.dma(lane(f"w4{j}"), (wh, wl)[j][:].bitcast(F32), (wh_d, wl_d)[j].rearrange("(k p) n -> p k n", p=128))
                   for j in range(2)]
            t_ub = [sp.dma(lane("ub"), ub[:, b, :], u_d[b, :].partition_broadcast(128)) for b in range(NB)][-1]
            t_gb = sp.dma(lane("gb4"), gb[:], gb_d[0, :].partition_broadcast(128))
            t_vp = [sp.dma(lane("vpb"), vpb[:, b, :], vp_d[b, :].partition_broadcast(128)) for b in range(NB)][-1]
            t_row = [sp.dma(lane("rows4"), rows[:, j, :], A[nm].partition_broadcast(128))
                     for j, nm in enumerate(("gamma", "beta"))][-1]
            for n in range(4, NX):
                load(n)
            ring = Banks(bank)
            tfree = [[] for _ in range(4)]
            gfree = [[] for _ in range(NG)]

            def chunk4(c):
                o = c % 4
                b = c // 2
                ts4, gs = [], []
                for i in range(4):
                    n = 4 * c + i
                    x = x3[n % NX]
                    g = gt[4 * o + i]
                    h = n % 4
                    bk, ps, bfree = ring.take()
                    for k in range(KT):
                        t = pe.op(lambda e, k=k, ps=ps, x=x: e.transpose(ps[:, 128 * k:128 * k + 128],
                                                                         x[:, 128 * k:128 * k + 128], ident[:]),
                                  bfree, X[n], inc=k == 3)
                    pv = ps.rearrange("p (k t) -> p k t", k=4)
                    a = act.op(lambda e, h=h, pv=pv: e.activation(th_[h][:], pv, ACT.Copy), t, tfree[h])
                    d = dve.op(lambda e, h=h, pv=pv: e.tensor_tensor(tl_[h][:], pv, th_[h][:].bitcast(F32), ALU.subtract),
                               a, tfree[h])
                    ring.free[bk] = [a, d]
                    yield
                    bk, ps, bfree = ring.take()
                    for k in range(KT):
                        t = three(ps, (th_[h][:, k, :], tl_[h][:, k, :]), (wh[:, k, :], wl[:, k, :]), k == 0, k == 3,
                                  bfree, d, t_w)
                    tfree[h] = [t]
                    r = rw[:, b, n % 8:n % 8 + 1]
                    d = dve.op(lambda e, g=g, r=r, ps=ps: e.scalar_tensor_tensor(g[:], ub[:, b, :], r, ps, ALU.mult, ALU.add),
                               t, R["rw", b], t_ub, gfree[4 * o + i])
                    ring.free[bk] = [d]
                    d = pool.op(lambda e, g=g: e.tensor_tensor(g[:], g[:], gb[:], ALU.add), d, t_gb)
                    yield
                    d = act.op(lambda e, g=g: e.activation(g[:], g[:], ACT.Sigmoid), d)
                    d = pool.op(lambda e, g=g: e.tensor_tensor(g[:], g[:], vpb[:, b, :], ALU.mult), d, t_vp)
                    yield
                    d = dve.op(lambda e, g=g, r=r, x=x: e.scalar_tensor_tensor(g[:], g[:], r, x[:], ALU.mult, ALU.add), d)
                    x3free[n % NX] = [d, t]
                    if n + NX < 32:
                        load(n + NX)
                    ts4.append(d)
                    gs.append(g[:])
                    yield
                mv, r_, tr = layer_stats(gs, ts4, small[:, c % 2, :])
                yield
                tn = normalise(gs, gs, ts4, mv, r_, tr)
                for i in range(4):
                    d = pool.op(lambda e, i=i: e.tensor_tensor(gs[i], gs[i], rows[:, 0, :], ALU.mult), tn[i], t_row)
                    d = dve.op(lambda e, i=i: e.tensor_tensor(gs[i], gs[i], rows[:, 1, :], ALU.add), d)
                    t0 = 512 * c + 128 * i
                    gfree[4 * o + i] = [sp.dma(lane(f"o{o}{i}"), out_d[t0:t0 + 128, :], gs[i], d)]
                    yield

            window([chunk4(c) for c in range(8)], 7, 3)
            sp.wait([(l[0], l[1]) for l in lanes.values()])

        for phase in (phase0, phase1, phase2, phase3, phase4):
            with ExitStack() as ctx:
                phase(ctx)

        block = top.enter_context(nc.Block())

        @block.tensor
        def _(e):
            pe.play(e)

        @block.scalar
        def _(e):
            act.play(e)

        @block.vector
        def _(e):
            dve.play(e)

        @block.gpsimd
        def _(e):
            pool.play(e)

        @block.sync
        def _(e):
            sp.play(e)


def kernel(**inputs):
    import numpy as _np
    import concourse.bacc as _bacc
    from concourse import mybir as _mybir
    from concourse.bass_utils import run_bass_kernel_spmd as _run

    f = {k[9:] if k.startswith("L") else k: _np.asarray(a) for k, a in inputs.items() if not k.startswith("L1")}
    g = {k[9:]: _np.asarray(a) for k, a in inputs.items() if k.startswith("L1")}
    heads = lambda w: w.transpose(1, 0, 2).reshape(512, 512)
    column = lambda v: v.reshape(-1, 128).T
    lay = {"x": f["x"], "ctxT": f["ctx_1024"].reshape(256, 512).T}
    stacked = lambda w: w.reshape(-1, 4, 4, 32).transpose(0, 1, 3, 2).reshape(-1, 512)
    for s in "sc":
        for n in "qkv":
            lay[f"W{n}_{s}"] = heads(f[f"W{n}_{s}"])
            lay[f"b{n}_{s}"] = f[f"b{n}_{s}"].reshape(512)
    for n in "qk":
        lay[f"W{n}_s"] = stacked(lay[f"W{n}_s"])
        lay[f"b{n}_s"] = stacked(lay[f"b{n}_s"])
    for n in ("bq_s", "bk_s", "bv_s", "bq_c", "bk_c"):
        lay[n] = column(lay[n])
    for n in ("g1", "be1", "g2", "be2", "g3", "be3", "bf1"):
        lay[n] = column(f[n])
    for n in ("W1", "W2", "Wf1", "Wf2", "b1", "b2", "bf2"):
        lay[n] = f[n]
    lay["bt"], lay["bv1"], lay["bv1r"] = column(g["bt"]), column(g["bv"]), g["bv"]
    lay["Wt"], lay["Wv1"], lay["Wg"] = g["Wt"], g["Wv"].T, g["Wg"].T
    for n in ("bg", "gamma", "beta"):
        lay[n] = g[n]

    nc = _bacc.Bacc("TRN2", target_bir_lowering=False, num_devices=1, dynamic_dma_scratch_size=1024)
    arrays, aps = {}, {}
    for n, a in lay.items():
        a = _np.ascontiguousarray(a)
        arrays[f"in_{n}"] = a
        aps[n] = nc.dram_tensor(f"in_{n}", a.shape, _mybir.dt.from_np(a.dtype), kind="ExternalInput").ap()
    out = nc.dram_tensor("out_0", (4, 1024, 512), _mybir.dt.float32, kind="ExternalOutput").ap()
    program(nc, aps, out)
    r = _run(nc, [arrays], core_ids=[0])
    return r.results[0]["out_0"]
```

```python
import numpy as np
import concourse.bass as bass
from concourse import mybir
from contextlib import ExitStack

F32 = mybir.dt.float32
F32R = mybir.dt.float32r
BF16 = mybir.dt.bfloat16
ALU = mybir.AluOpType
ACT = mybir.ActivationFunctionType
AX = mybir.AxisListType.X

NB, T, C, H, DH = 4, 1024, 512, 16, 32
S = 64
KT = 4
EPS = 1e-5
SCALE = 1.0 / (DH ** -0.5)
NEG = -1e30
LN_GAP = (10, 10, 6)
MX_GAP = 2
MAX_TOTAL = 65
LATE = 2
W_AT = 0
NRAW = 4
CH_GAP = (4, 10, 16, 6)


class Queue:

    def __init__(self, sem):
        self.sem, self.n, self.items, self.seen = sem, 0, [], {}

    def wait(self, *tokens):
        for t in tokens:
            if isinstance(t, list):
                self.wait(*t)
            elif t is not None and self.seen.get(id(t[0]), 0) < t[1]:
                self.seen[id(t[0])] = t[1]
                self.items.append((None, t[0], t[1]))

    def op(self, fn, *tokens, inc=True):
        self.wait(*tokens)
        if not inc:
            self.items.append((fn, None, 0))
            return None
        self.n += 1
        self.items.append((fn, self.sem, 1))
        return (self.sem, self.n)

    def dma(self, lane, out, in_, *tokens):
        self.wait(*tokens)
        lane[1] += 16
        self.items.append((lambda e, o=out, i=in_: e.dma_start(o, i), lane[0], 16))
        return (lane[0], lane[1])

    def last(self):
        return (self.sem, self.n)

    def play(self, eng):
        for fn, sem, n in self.items:
            if fn is None:
                eng.wait_ge(sem, n)
            elif sem is None:
                fn(eng)
            else:
                fn(eng).then_inc(sem, n)


class Banks:

    def __init__(self, aps, group=1):
        self.aps, self.free, self.at = aps, [[] for _ in aps], 0

    def take(self):
        i = self.at % len(self.aps)
        self.at += 1
        return i, self.aps[i], self.free[i]


def merge(*streams):
    live = [[g, total, 0.0] for g, total in streams]
    while live:
        s = min(live, key=lambda s: s[2] / s[1])
        cost = next(s[0], None)
        if cost is None:
            live.remove(s)
        else:
            s[2] += cost


def window(gens, lag, width=2):
    live = []
    gens = list(gens)
    while gens or live:
        if gens and (not live or (len(live) < width and live[-1][1] >= lag)):
            live.append([gens.pop(0), 0])
        for g in list(live):
            g[1] += 1
            if next(g[0], StopIteration) is StopIteration:
                live.remove(g)


def program(nc, A, out):
    top = ExitStack()
    with top:
        sem = lambda n: top.enter_context(nc.semaphore(n))
        pe, act, dve, pool, sp = [Queue(sem(n)) for n in ("s_pe", "s_act", "s_dve", "s_pool", "s_sp")]
        engines = [pe, act, dve, pool]
        lanes = {}

        def lane(name):
            if name not in lanes:
                lanes[name] = [sem("d_" + name), 0]
            return lanes[name]

        def sb(ctx, name, shape, dt=F32):
            return ctx.enter_context(nc.sbuf_tensor(name, shape, dt))

        psum = top.enter_context(nc.psum_tensor("psum", [128, 8, 512], F32))
        bank = [psum[:, i, :] for i in range(8)]

        sa_d = nc.dram_tensor("sa_d", [C, NB * T], F32, kind="Internal").ap()
        x2_d = nc.dram_tensor("x2_d", [NB * T, C], F32, kind="Internal").ap()
        x3_d = nc.dram_tensor("x3_d", [NB * T, C], F32, kind="Internal").ap()
        wh_d = nc.dram_tensor("wh_d", [C, C], F32, kind="Internal").ap()
        wl_d = nc.dram_tensor("wl_d", [C, C], F32, kind="Internal").ap()
        vp_d = nc.dram_tensor("vp_d", [NB, C], F32, kind="Internal").ap()
        wvp_d = nc.dram_tensor("wvp_d", [NB, C], F32, kind="Internal").ap()
        u_d = nc.dram_tensor("u_d", [NB, C], F32, kind="Internal").ap()
        gb_d = nc.dram_tensor("gb_d", [1, C], F32, kind="Internal").ap()
        cb_d = nc.dram_tensor("cb_d", [NB, 1], F32, kind="Internal").ap()
        x_d = A["x"].rearrange("b t c -> (b t) c")
        out_d = out.rearrange("b t c -> (b t) c")
        stores = {}

        ident = sb(top, "ident", [128, 128])
        identb = sb(top, "identb", [128, 128], BF16)
        mask_ts = sb(top, "mask_ts", [128, 128], BF16)
        mask_st = sb(top, "mask_st", [128, 128], BF16)
        cols = sb(top, "cols", [128, 68])
        small = sb(top, "small", [128, 2, 128])
        ag = sb(top, "ag", [128, NB, 8])
        rw = sb(top, "rw", [128, NB, 8])
        sm4 = sb(top, "sm4", [128, NB, 8])
        cb = sb(top, "cb", [128, NB])
        R = {}

        z = pool.op(lambda e: e.memset(ident[:], 0.0))
        t_ident = pool.op(lambda e: e.affine_select(out=ident[:], in_=ident[:], compare_op=ALU.not_equal, fill=1.0,
                                                    base=0, pattern=[[-1, 128]], channel_multiplier=1), z)
        z1 = pool.op(lambda e: e.memset(mask_ts[:], 0.0))
        z2 = pool.op(lambda e: e.memset(mask_st[:], 0.0))
        t_m1 = pool.op(lambda e: e.affine_select(out=mask_ts[:], in_=mask_ts[:], compare_op=ALU.is_ge, fill=NEG,
                                                 base=0, pattern=[[-1, 128]], channel_multiplier=1), z1)
        t_m2 = pool.op(lambda e: e.affine_select(out=mask_st[:], in_=mask_st[:], compare_op=ALU.is_ge, fill=NEG,
                                                 base=0, pattern=[[1, 128]], channel_multiplier=-1), z2)
        t_identb = dve.op(lambda e: e.tensor_copy(identb[:], ident[:]), t_ident)
        t_consts = [t_ident, t_identb, t_m1, t_m2]

        col_at = {}
        n = 0
        for name, width in (("g1", 4), ("be1", 4), ("g2", 4), ("be2", 4), ("g3", 4), ("be3", 4), ("bq_s", 4),
                            ("bk_s", 4), ("bq_c", 4), ("bk_c", 4), ("bf1", 16), ("bt", 4), ("bv1", 4), ("bv_s", 4)):
            col_at[name] = n
            t_cols = sp.dma(lane("cols"), cols[:, n:n + width], A[name])
            n += width

        def col(name, k):
            return cols[:, col_at[name] + k:col_at[name] + k + 1]

        def fence():
            done = [q.last() for q in engines if q.n] + [(l[0], l[1]) for l in lanes.values()]
            for q in engines + [sp]:
                q.wait(done)

        def split_weight(src, raw, raw_free, hi, lo, ln):
            t = sp.dma(lane(ln), raw, src.rearrange("(k p) n -> p k n", p=128), raw_free)
            a = act.op(lambda e: e.activation(hi, raw, ACT.Copy), t)
            d = dve.op(lambda e: e.tensor_tensor(lo, raw, hi.bitcast(F32), ALU.subtract), t, a)
            return [a, d]

        def three(dst, lhs, rhs, start, stop, *tokens):
            pe.wait(*tokens)
            (lh, ll), (rh, rl) = lhs, rhs
            pe.op(lambda e: e.matmul(dst, lh, rh, start=start, stop=False), inc=False)
            pe.op(lambda e: e.matmul(dst, lh, rl, start=False, stop=False), inc=False)
            return pe.op(lambda e: e.matmul(dst, ll, rh, start=False, stop=stop), inc=stop)

        def layer_stats(xs, toks, sm):
            nt = len(xs)
            mv = sm[:, 64:64 + 2 * nt].rearrange("p (t a) -> p t a", a=2)
            st = sm[:, 0:6 * nt].rearrange("p (t a) -> p t a", a=6)
            ta = []
            for i, x in enumerate(xs):
                ta.append(dve.op(lambda e, i=i, x=x: e.bn_stats(st[:, i, :], x), toks[i]))
            tb = [dve.op(lambda e, i=i: e.bn_aggr(mv[:, i, :], st[:, i, :]), ta[i]) for i in range(nt)]
            v, r, u = (sm[:, 96 + 8 * j:96 + 8 * j + nt] for j in range(3))
            t = dve.op(lambda e: e.tensor_scalar(v, mv[:, :, 1], EPS, None, ALU.add), tb)
            t = act.op(lambda e: e.activation(u, v, ACT.Sqrt), t)
            t = dve.op(lambda e: e.reciprocal(r, u), t)
            t = dve.op(lambda e: e.tensor_tensor(u, r, r, ALU.mult), t)
            t = dve.op(lambda e: e.tensor_tensor(u, u, v, ALU.mult), t)
            t = dve.op(lambda e: e.tensor_scalar(u, u, -0.5, 1.5, ALU.mult, ALU.add), t)
            t = dve.op(lambda e: e.tensor_tensor(r, r, u, ALU.mult), t)
            return mv, r, t

        def normalise(xs, outs, toks, mv, r, t):
            got = []
            for i, (x, o) in enumerate(zip(xs, outs)):
                got.append(dve.op(lambda e, i=i, x=x, o=o: e.tensor_scalar(
                    o, x, mv[:, i, 0:1], r[:, i:i + 1], ALU.subtract, ALU.mult), t, toks[i]))
            return got

        def transposed(xs, toks, ring, ys, yfree, g, be, hi, lo, free):
            nt = len(xs)
            got, last = [], None
            for k in range(KT):
                b, ps, bfree = ring.take()
                for i, x in enumerate(xs):
                    t = pe.op(lambda e, i=i, x=x, ps=ps, k=k: e.transpose(
                        ps[:, 128 * i:128 * i + 128], x[:, 128 * k:128 * k + 128], ident[:]),
                        bfree, toks[i], t_ident, inc=i == nt - 1)
                last = t
                y = ys[k % 2][:, 0:128 * nt]
                t = act.op(lambda e, y=y, ps=ps, k=k: e.activation(
                    y, ps[:, 0:128 * nt], ACT.Identity, bias=col(be, k), scale=col(g, k)), t, yfree[k % 2], t_cols)
                ring.free[b] = [t]
                a = dve.op(lambda e, y=y, k=k: e.tensor_copy(hi[:, k, :], y), t, free)
                d = dve.op(lambda e, y=y, k=k: e.tensor_tensor(
                    lo[:, k, :], y, hi[:, k, :].bitcast(F32), ALU.subtract), a, t)
                yfree[k % 2] = [d]
                got.append(d)
                yield None
            yield got, last

        def phase0(ctx):
            wt = sb(ctx, "wt", [128, KT, C])
            wg = sb(ctx, "wg", [128, 8, C])
            wv = sb(ctx, "wv1", [128, KT, C])
            wh = sb(ctx, "wh", [128, KT, C], F32R)
            wl = sb(ctx, "wl", [128, KT, C], F32R)
            ct = sb(ctx, "ct4", [128, KT, NB, S])
            pl = sb(ctx, "pl", [128, KT, NB])
            vcol = sb(ctx, "vcol", [128, KT, NB])
            rows = sb(ctx, "rows", [NB, 2, C])
            orow = [sb(ctx, f"orow{i}", [NB, C]) for i in range(4)]
            ocb = sb(ctx, "ocb", [NB, 1])
            t_row = [sp.dma(lane("rows"), rows[0:NB, j, :], A[nm].partition_broadcast(NB))
                     for j, nm in enumerate(("bv1r", "bg"))][-1]
            t_ct = sp.dma(lane("ct"), ct[:], A["ctxT"].rearrange("(k p) (b s) -> p k b s", p=128, s=S))
            t_wv = sp.dma(lane("wv"), wv[:], A["Wv1"].rearrange("(k p) n -> p k n", p=128))
            t_wt = sp.dma(lane("wk"), wt[:], A["Wt"].rearrange("(k p) n -> p k n", p=128))
            t_wg = sp.dma(lane("bvc"), wg[:], A["Wg"].rearrange("(k p) n -> p k n", p=128))
            d0 = dve.op(lambda e: e.tensor_reduce(pl[:], ct[:], AX, ALU.add), t_ct)
            d1 = dve.op(lambda e: e.tensor_scalar(pl[:], pl[:], 1.0 / S, None, ALU.mult), d0)
            bt = cols[:, col_at["bt"]:col_at["bt"] + 4]
            ring = Banks(bank)

            def native(m, n, lhs, rhs, *tokens):
                b, ps, bfree = ring.take()
                for k in range(KT):
                    t = pe.op(lambda e, k=k, ps=ps: e.matmul(ps[0:m, 0:n], lhs(k), rhs(k), start=k == 0, stop=k == 3),
                              bfree, *tokens, inc=k == 3)
                return b, ps, t

            tv = []
            for m in range(4):
                b, ps, t = native(128, NB, lambda k, m=m: wv[:, k, 128 * m:128 * m + 128], lambda k: pl[:, k, :], t_wv, d1)
                d = dve.op(lambda e, m=m, ps=ps: e.tensor_scalar(vcol[:, m, :], ps[:, 0:NB], col("bv1", m), None, ALU.add), t, t_cols)
                ring.free[b] = [d]
                tv.append(d)
            b, ps, t = native(NB, C, lambda k: pl[:, k, :], lambda k: wv[:, k, :], t_wv, d1)
            d = dve.op(lambda e, ps=ps: e.tensor_tensor(orow[0][:], ps[0:NB, :], rows[:, 0, :], ALU.add), t, t_row)
            ring.free[b] = [d]
            sp.dma(lane("vp"), vp_d, orow[0][:], d)
            b, ps, t = native(NB, C, lambda k: vcol[:, k, :], lambda k: wt[:, k, :], tv, t_wt)
            a = act.op(lambda e, ps=ps: e.activation(orow[1][:], ps[0:NB, :], ACT.Copy), t)
            ring.free[b] = [a]
            sp.dma(lane("wvp"), wvp_d, orow[1][:], a)
            b, ps, t = native(NB, C, lambda k: vcol[:, k, :], lambda k: wg[:, 4 + k, :], tv, t_wg)
            a = act.op(lambda e, ps=ps: e.activation(orow[2][:], ps[0:NB, :], ACT.Copy), t)
            ring.free[b] = [a]
            sp.dma(lane("u"), u_d, orow[2][:], a)
            b, ps, t = native(NB, 1, lambda k: vcol[:, k, :], lambda k: bt[:, k:k + 1], tv, t_cols)
            a = act.op(lambda e, ps=ps: e.activation(ocb[:], ps[0:NB, 0:1], ACT.Copy), t)
            ring.free[b] = [a]
            sp.dma(lane("cb"), cb_d, ocb[:], a)
            b, ps, t = native(1, C, lambda k: bt[:, k:k + 1], lambda k: wg[:, k, :], t_cols, t_wg)
            d = dve.op(lambda e, ps=ps: e.tensor_tensor(orow[3][0:1, :], ps[0:1, :], rows[0:1, 1, :], ALU.add), t, t_row)
            ring.free[b] = [d]
            sp.dma(lane("gb"), gb_d, orow[3][0:1, :], d)
            for m in range(4):
                b, ps, t = native(128, C, lambda k, m=m: wt[:, k, 128 * m:128 * m + 128], lambda k: wg[:, k, :], t_wt, t_wg)
                a = act.op(lambda e, m=m, ps=ps: e.activation(wh[:, m, :], ps, ACT.Copy), t)
                d = dve.op(lambda e, m=m, ps=ps: e.tensor_tensor(wl[:, m, :], ps, wh[:, m, :].bitcast(F32), ALU.subtract), a)
                ring.free[b] = [a, d]
                sp.dma(lane("whl"), wh_d[128 * m:128 * m + 128, :], wh[:, m, :].bitcast(F32), a)
                sp.dma(lane("whl"), wl_d[128 * m:128 * m + 128, :], wl[:, m, :].bitcast(F32), d)
            fence()

        def phase1(ctx):
            W = {}
            for nm in ("q", "k", "v"):
                W[nm] = (sb(ctx, f"w{nm}h", [128, KT, C], F32R), sb(ctx, f"w{nm}l", [128, KT, C], F32R))
            er = sb(ctx, "er", [128, 8, 512])
            xr = sb(ctx, "xr", [128, 2, 512])
            ys = [sb(ctx, f"y{i}", [128, 256]) for i in range(2)]
            xh = sb(ctx, "xh", [128, KT, T], F32R)
            xl = sb(ctx, "xl", [128, KT, T], F32R)
            v = sb(ctx, "v", [128, 8, C])
            stage = [sb(ctx, f"stage{i}", [128, T], F32R) for i in range(4)]
            qs = [sb(ctx, f"qs{p}", [128, 4, T], F32R) for p in range(2)]
            ks = [sb(ctx, f"ks{p}", [128, 4, T], F32R) for p in range(2)]
            esum = [[sb(ctx, f"es{o}{i}", [128, 512]) for i in range(4)] for o in range(2)]
            sao = [sb(ctx, f"sao{o}", [128, 512]) for o in range(2)]
            mx = sb(ctx, "mx", [128, 176])
            ones = sm4[:].rearrange("p b e -> p (b e)")

            t_ones = dve.op(lambda e: e.memset(ones, 1.0))
            t_mx0 = pool.op(lambda e: e.memset(mx[:], 0.0))
            oh = esum[0][0][96:128, 0:512].rearrange("p (i n) -> p i n", i=4)
            t = pool.op(lambda e: e.memset(oh, 0.0), t_mx0)
            t = pool.op(lambda e: e.affine_select(out=oh, in_=oh, compare_op=ALU.not_equal, fill=1.0, base=0,
                                                  pattern=[[-1, 4], [0, 128]], channel_multiplier=1), t)
            pool.wait(t)
            t_oh = [dve.op(lambda e, p=p, q=q: e.tensor_copy(
                ks[p][96:128, :, 128 * q:128 * q + 128], oh), t) for p in range(2) for q in range(8)]
            tw, rf = {}, [[], []]
            for j, nm in enumerate(("q", "k", "v")):
                tw[nm] = split_weight(A[f"W{nm}_s"], er[:, 4 * (j % 2):4 * (j % 2) + 4, :], rf[j % 2],
                                      W[nm][0][:], W[nm][1][:], f"raw{j % 2}")
                rf[j % 2] = tw[nm]

            ringB = Banks(bank[0:2])
            ringM = Banks(bank[2:4])
            ringS = Banks(bank[4:7])
            ringO = Banks(bank[7:8])
            xfree = [[], []]
            yfree = [[], []]
            xhfree, vfree, stfree = [], [], []
            stack_free = [[], []]
            efree = [list(rf[i // 4]) for i in range(8)]
            esfree = [[[t_oh] for _ in range(4)] for _ in range(2)]
            saofree = [[], []]
            mxfree = [t_mx0]
            state = {"e": 0, "o": 0, "fin": None}

            def gen_ln(b):
                got = []

                def load(qt):
                    return [sp.dma(lane(f"x{i}"), xr[:, i, :],
                                   x_d[b * T + qt * 256 + i * 128:b * T + qt * 256 + (i + 1) * 128, :], xfree[i])
                            for i in range(2)]

                toks = load(0)
                for qt in range(4):
                    yield LN_GAP[0]
                    xs = [xr[:, i, :] for i in range(2)]
                    mv, r, t = layer_stats(xs, toks, small[:, 0, :])
                    yield LN_GAP[1]
                    tn = normalise(xs, xs, toks, mv, r, t)
                    yield LN_GAP[2]
                    ts = slice(256 * qt, 256 * qt + 256)
                    for step in transposed(xs, tn, ringB, ys, yfree, "g1", "be1", xh[:, :, ts], xl[:, :, ts], xhfree):
                        if step is None:
                            yield 1
                        else:
                            got.append(step[0])
                            for i in range(2):
                                xfree[i] = [step[1]]
                    if qt < 3:
                        toks = load(qt + 1)
                state["xn", b] = got

            def gen_proj(g):
                b, gg = divmod(g, 4)
                got = {}
                for c2 in range(2):
                    for w, nm in enumerate(("q", "k")):
                        bk, ps, bfree = ringB.take()
                        cs = slice(128 * gg, 128 * gg + 128)
                        ts = slice(512 * c2, 512 * c2 + 512)
                        for k in range(KT):
                            t = three(ps, (W[nm][0][:, k, cs], W[nm][1][:, k, cs]), (xh[:, k, ts], xl[:, k, ts]),
                                      k == 0, k == KT - 1, bfree, tw[nm], state["xn", b][2 * c2][k],
                                      state["xn", b][2 * c2 + 1][k])
                            yield 3
                        hi, lo = stage[2 * w][:, ts], stage[2 * w + 1][:, ts]
                        bias = col(f"b{nm}_s", gg)
                        a = act.op(lambda e, hi=hi, ps=ps, bias=bias: e.activation(
                            hi, ps, ACT.Identity, bias=bias, scale=1.0), t, stfree, t_cols)
                        yield LATE
                        d = dve.op(lambda e, hi=hi, lo=lo, ps=ps, bias=bias: e.scalar_tensor_tensor(
                            lo, ps, bias, hi.bitcast(F32), ALU.add, ALU.subtract), a, stfree)
                        ringB.free[bk] = [a, d]
                        got[w, c2] = [a, d]
                state["stage", g] = got
                if gg == 3:
                    xhfree[:] = [t]

            def stack(g):
                par = g % 2
                tl = {}
                for c2 in range(2):
                    ts = slice(512 * c2, 512 * c2 + 512)
                    for w, order in ((0, (0, 1, 0)), (1, (0, 0, 1))):
                        for r, part in enumerate(order):
                            tl[w, c2] = sp.dma(lane(f"stk{par}{w}{c2}"),
                                               (qs, ks)[w][par][32 * r:32 * r + 32, :, ts].bitcast(F32),
                                               stage[2 * w + part][:, ts].bitcast(F32),
                                               state["stage", g][w, c2], stack_free[par])
                stfree[:] = list(tl.values())
                state["stack", g] = tl

            def gen_max(g):
                par = g % 2
                tl = state["stack", g]
                tm = []
                yield 8
                for ti in range(8):
                    wd = 128 * (ti + 1)
                    per = 4 if ti == 0 else 2 if ti == 1 else 1
                    for h0 in range(0, 4, per):
                        for c0 in range(0, wd, 512):
                            w = min(512, wd - c0)
                            diag = c0 + w == wd
                            bk, ps, bfree = ringM.take()
                            for u in range(per):
                                i = h0 + u
                                q = qs[par][0:96, i, 128 * ti:128 * ti + 128]
                                t = pe.op(lambda e, q=q, i=i, u=u, w=w, c0=c0, ps=ps, diag=diag: e.matmul(
                                    ps[:, u * w:u * w + w], q, ks[par][0:96, i, c0:c0 + w], start=True, stop=not diag),
                                    [tl[0, ti // 4], tl[1, c0 // 512]], bfree, inc=not diag)
                                if diag:
                                    t = pe.op(lambda e, u=u, w=w, ps=ps: e.matmul(
                                        ps[:, u * w + w - 128:u * w + w], identb[:], mask_ts[:], start=False, stop=True),
                                        t_consts, inc=u == per - 1)
                            src = ps[:, 0:per * w].rearrange("p (u n) -> p u n", u=per)
                            at = 4 * ti + h0 + (96 if diag else 160 - 16)
                            d = dve.op(lambda e, at=at, per=per, src=src: e.tensor_reduce(
                                mx[:, at:at + per], src, AX, ALU.max, negate=True), t, mxfree)
                            ringM.free[bk] = [d]
                            tm.append(d)
                            yield per * (w + 128 * diag) / 512
                tm = [dve.op(lambda e: e.tensor_tensor(mx[:, 112:128], mx[:, 112:128], mx[:, 160:176], ALU.min), tm)]
                yield MX_GAP
                tq = []
                for c2 in range(2):
                    bk, ps, bfree = ringM.take()
                    for ti in range(4 * c2, 4 * c2 + 4):
                        t = pe.op(lambda e, ti=ti, ps=ps: e.transpose(
                            ps[:, 128 * (ti % 4):128 * (ti % 4) + 128], mx[:, 4 * ti:4 * ti + 128], ident[:]),
                            tm, bfree, t_ident, inc=ti % 4 == 3)
                    tc = [act.op(lambda e, i=i, ps=ps, c2=c2: e.activation(
                        qs[par][96:128, i, 512 * c2:512 * c2 + 512], ps[96:128, :], ACT.Copy),
                        t, stack_free[par]) for i in range(4)]
                    ringM.free[bk] = [tc[3]]
                    tq.append(tc)
                    yield 2
                mxfree[:] = [t]
                state["max", g] = tq

            def gen_v(b):
                got = []
                for st in range(8):
                    bk, ps, bfree = ringS.take()
                    for k in range(KT):
                        ss = slice(128 * st, 128 * st + 128)
                        t = three(ps, (xh[:, k, ss], xl[:, k, ss]), (W["v"][0][:, k, :], W["v"][1][:, k, :]),
                                  k == 0, k == KT - 1, bfree, tw["v"], state["xn", b][st // 2][k])
                        yield 3
                    d = act.op(lambda e, ps=ps, st=st: e.activation(v[:, st, :], ps, ACT.Copy), t, vfree)
                    ringS.free[bk] = [d]
                    got.append(d)
                    if st == 3:
                        for _ in finish():
                            pass
                state["v", b] = got

            def finish():
                if state["fin"] is None:
                    return
                g, c2, o, t_o, tsum = state["fin"]
                state["fin"] = None
                b, gg = divmod(g, 4)
                sbk, ps, sfree = ringS.take()
                for i in range(4):
                    t = pe.op(lambda e, i=i, ps=ps: e.matmul(ps[32 * i:32 * i + 32, :], ones, esum[o][i][:],
                                                             start=True, stop=True), tsum[i], sfree, t_ones)
                    esfree[o][i] = [t]
                ssb = esum[o][0]
                a = act.op(lambda e, ps=ps: e.activation(ssb[:], ps, ACT.Copy), t)
                ringS.free[sbk] = [a]
                yield
                td = []
                for q in range(4):
                    r = slice(128 * q, 128 * q + 128)
                    d = dve.op(lambda e, r=r: e.reciprocal(ssb[:, r], ssb[:, r]), a)
                    td.append(dve.op(lambda e, r=r: e.tensor_tensor(sao[o][:, r], sao[o][:, r], ssb[:, r], ALU.mult), d, t_o))
                    if q < 3:
                        yield
                esfree[o][0] = [td[-1]]
                t0 = b * T + c2 * 512
                saofree[o][:] = [sp.dma(lane(f"sa{o}"), sa_d[128 * gg:128 * gg + 128, t0:t0 + 512], sao[o][:], td)]
                yield

            def gen_a(g):
                b, gg = divmod(g, 4)
                par = g % 2
                if gg == 0:
                    yield from gen_v(b)
                tv = state["v", b]
                tl, tq = state["stack", g], state["max", g]
                for c2 in range(2):
                    o = state["o"] % 2
                    state["o"] += 1
                    ob, po, ofree = ringO.take()
                    nj = 4 * c2 + 4
                    tsum = [None] * 4
                    pending = []
                    fin = finish()

                    def products(i, jj, off, dst, slot, x, po, nj, o):
                        t = pe.op(lambda e: e.matmul(
                            po[32 * i:32 * i + 32, off:512], v[:, jj, 128 * gg + 32 * i:128 * gg + 32 * i + 32],
                            dst[:, off:512], start=jj == 0, stop=jj == nj - 1), x, tv[jj], ofree)
                        if jj == 0:
                            tsum[i] = t
                        else:
                            tsum[i] = pool.op(lambda e: e.tensor_tensor(
                                esum[o][i][:, off:512], esum[o][i][:, off:512], dst[:, off:512], ALU.add), tsum[i], x)
                            efree[slot] = [tsum[i], t]
                        return t

                    for j in range(nj):
                        off = max(0, 128 * (j - 4 * c2))
                        for i in range(4):
                            sbk, ps, sfree = ringS.take()
                            t = pe.op(lambda e, i=i, j=j, ps=ps, off=off, c2=c2: e.matmul(
                                ps[:, off:512], ks[par][:, i, 128 * j:128 * j + 128],
                                qs[par][:, i, 512 * c2 + off:512 * c2 + 512], start=True, stop=j < 4 * c2),
                                sfree, [tl[0, c2], tl[1, 0]] + ([tl[1, 1]] if j >= 4 else []), tq[c2][i], t_oh, inc=j < 4 * c2)
                            if j >= 4 * c2:
                                t = pe.op(lambda e, ps=ps, off=off: e.matmul(
                                    ps[:, off:off + 128], identb[:], mask_st[:], start=False, stop=True), t_consts)
                            if j == 0:
                                dst, free, slot = esum[o][i], esfree[o][i], None
                            else:
                                slot = state["e"] % 8
                                state["e"] += 1
                                dst, free = er[:, slot, :], efree[slot]
                            x = act.op(lambda e, dst=dst, ps=ps, off=off: e.activation(
                                dst[:, off:512], ps[:, off:512], ACT.Exp, scale=SCALE), t, free)
                            ringS.free[sbk] = [x]
                            pending.append((i, j, off, dst, slot, x))
                            yield 1.2 * (512 - off) / 512
                            if j >= 2:
                                next(fin, None)
                            if i == 3 and len(pending) > 4:
                                for _ in range(4):
                                    tpv = products(*pending.pop(0), po, nj, o)
                                yield 4 * (512 - off) / 512
                    while pending:
                        tpv = products(*pending.pop(0), po, nj, o)
                    yield 1
                    t_o = act.op(lambda e, po=po, o=o: e.activation(sao[o][:], po, ACT.Copy), tpv, saofree[o])
                    ringO.free[ob] = [t_o]
                    state["fin"] = (g, c2, o, t_o, tsum)
                stack_free[par][:] = [t]
                if gg == 3:
                    vfree[:] = [tpv]

            def chain(*gens):
                for x in gens:
                    yield from x

            for x in chain(gen_ln(0), gen_proj(0)):
                pass
            stack(0)
            for x in chain(gen_proj(1), gen_max(0)):
                pass
            for g in range(16):
                todo = [(gen_a(g), 88 + (96 if g % 4 == 0 else 0))]
                if g < 15:
                    stack(g + 1)
                    todo.append((gen_max(g + 1), MAX_TOTAL))
                if g + 2 < 16:
                    if (g + 2) % 4 == 0:
                        todo.append((chain(gen_ln((g + 2) // 4), gen_proj(g + 2)), 64 + 4 * sum(LN_GAP) + 4 * LATE))
                    else:
                        todo.append((gen_proj(g + 2), 48 + 4 * LATE))
                merge(*todo)
            for _ in finish():
                pass
            fence()

        def phase2(ctx):
            W = {}
            for nm in ("W1", "Wq_c", "W2"):
                W[nm] = (sb(ctx, f"{nm}h", [128, KT, C], F32R), sb(ctx, f"{nm}l", [128, KT, C], F32R))
            kbh = sb(ctx, "kbh", [128, NB, 4, 256], F32R)
            kbl = sb(ctx, "kbl", [128, NB, 4, 256], F32R)
            vb = sb(ctx, "vb", [128, NB, C])
            b1b = sb(ctx, "b1b", [128, C])
            b2b = sb(ctx, "b2b", [128, C])
            xt = [sb(ctx, f"xt{p}", [128, 4, C]) for p in range(3)]
            sx = sb(ctx, "sx", [128, 4, C])
            ah = sb(ctx, "ah", [128, KT, 512], F32R)
            al = sb(ctx, "al", [128, KT, 512], F32R)
            qh = [sb(ctx, f"qh{p}", [128, 4, 512], F32R) for p in range(2)]
            ql = [sb(ctx, f"ql{p}", [128, 4, 512], F32R) for p in range(2)]
            pp = [sb(ctx, f"pp{p}", [128, 16, S]) for p in range(2)]
            pT = [sb(ctx, f"pT{p}", [128, 8, 128]) for p in range(2)]
            ch = [sb(ctx, f"ch{p}", [128, 4, 128], F32R) for p in range(2)]
            cl = [sb(ctx, f"cl{p}", [128, 4, 128], F32R) for p in range(2)]
            ys = [sb(ctx, f"y2{i}", [128, 512]) for i in range(2)]

            tw, rfree = {}, [[], []]
            raws = [xt[1][:], xt[2][:]]

            def weight(j, nm):
                tw[nm] = split_weight(A[nm], raws[j], rfree[j], W[nm][0][:], W[nm][1][:], f"raw{j}")
                rfree[j] = tw[nm]

            weight(0, "W1")
            weight(1, "Wq_c")
            t_b1 = sp.dma(lane("b1"), b1b[:], A["b1"].partition_broadcast(128))
            t_b2 = sp.dma(lane("b2"), b2b[:], A["b2"].partition_broadcast(128))
            nm_ = [sb(ctx, f"nm{p}", [128, 16]) for p in range(2)]
            sm_ = [sb(ctx, f"sm{p}", [128, 16]) for p in range(2)]

            ringI = Banks(bank[0:3])
            xfree = [[[] for _ in range(4)] for _ in range(3)]
            F = {"s": [], "a": [], "y": [[], []], "q": [[], []]}
            Q, X = {}, {}

            def chunk(c):
                p, b = c % 3, c // 2
                t0 = 512 * c
                xs = [xt[p][:, i, :] for i in range(4)]
                ts_ = sp.dma(lane("cs"), sx[:], sa_d[:, t0:t0 + 512].rearrange("(k p) n -> p k n", p=128), F["s"])
                tx = [sp.dma(lane(f"cx{p}{i}"), xs[i], x_d[t0 + 128 * i:t0 + 128 * i + 128, :], xfree[p][i]) for i in range(4)]
                yield CH_GAP[0]
                tsp = []
                for k in range(KT):
                    a = act.op(lambda e, k=k: e.activation(ah[:, k, :], sx[:, k, :], ACT.Identity, bias=col("bv_s", k),
                                                           scale=1.0), ts_, F["a"])
                    tsp.append(dve.op(lambda e, k=k: e.scalar_tensor_tensor(
                        al[:, k, :], sx[:, k, :], col("bv_s", k), ah[:, k, :].bitcast(F32), ALU.add, ALU.subtract), a))
                tb = [pool.op(lambda e, i=i: e.tensor_tensor(xs[i], xs[i], b1b[:], ALU.add), tx[i], t_b1) for i in range(4)]
                yield CH_GAP[1]
                t1 = []
                for i in range(4):
                    bk, ps, bfree = ringI.take()
                    r = slice(128 * i, 128 * i + 128)
                    for k in range(KT):
                        t = three(ps, (ah[:, k, r], al[:, k, r]), (W["W1"][0][:, k, :], W["W1"][1][:, k, :]),
                                  k == 0, k == 3, bfree, tsp[k], tw["W1"])
                        yield 3
                    d = dve.op(lambda e, i=i, ps=ps: e.tensor_tensor(xs[i], ps, xs[i], ALU.add), t, tb[i])
                    ringI.free[bk] = [d]
                    t1.append(d)
                ta = t
                mv, r_, tr = layer_stats(xs, t1, small[:, 0, :])
                yield CH_GAP[2]
                xn = [sx[:, i, :] for i in range(4)]
                tn = normalise(xs, xn, t1, mv, r_, tr)
                X[c] = [pool.op(lambda e, i=i: e.tensor_tensor(xs[i], xs[i], b2b[:], ALU.add), tn[i], t_b2) for i in range(4)]
                yield CH_GAP[3]
                for step in transposed(xn, tn, ringI, ys, F["y"], "g2", "be2", ah, al, [ta]):
                    if step is None:
                        yield 2
                    else:
                        txn, tl = step
                F["s"] = [tl]
                tq = []
                qp = c % 2
                for m in range(4):
                    bk, ps, bfree = ringI.take()
                    for k in range(KT):
                        t = three(ps, tuple(W["Wq_c"][j][:, k, 128 * m:128 * m + 128] for j in range(2)),
                                  (ah[:, k, :], al[:, k, :]), k == 0, k == 3, bfree, txn[k], tw["Wq_c"])
                        yield 3
                    a = act.op(lambda e, m=m, ps=ps: e.activation(qh[qp][:, m, :], ps, ACT.Identity, bias=col("bq_c", m),
                                                                  scale=1.0), t, F["q"][qp])
                    d = dve.op(lambda e, m=m, ps=ps: e.scalar_tensor_tensor(
                        ql[qp][:, m, :], ps, col("bq_c", m), qh[qp][:, m, :].bitcast(F32), ALU.add, ALU.subtract),
                        a, F["q"][qp])
                    ringI.free[bk] = [a, d]
                    tq.append(d)
                F["a"] = [t]
                Q[c] = tq

            ringP = Banks(bank[3:5])
            ringT = Banks(bank[5:8])
            wkv = [sb(ctx, "wkv", [128, KT, C])]
            ct = sb(ctx, "ctc", [128, KT, 256])
            bvc = pT[0][:].rearrange("p a n -> p (a n)")[:, 0:512]
            t_ct = sp.dma(lane("ct"), ct[:], A["ctxT"].rearrange("(k p) n -> p k n", p=128))
            t_wk = sp.dma(lane("wk"), wkv[0][:], A["Wk_c"].rearrange("(k p) n -> p k n", p=128))
            t_bvc = sp.dma(lane("bvc"), bvc, A["bv_c"].partition_broadcast(128))
            tz = [pool.op(lambda e, q=q: e.memset(q, 0.0)) for q in (kbh[:].bitcast(F32), kbl[:].bitcast(F32), vb[:])]
            cd = [pp[0][:].rearrange("p h s -> p (h s)"), pp[1][:].rearrange("p h s -> p (h s)")]
            td = [dve.op(lambda e, k=k, j=j: e.tensor_copy(
                cd[k // 2][:, 512 * (k % 2):512 * (k % 2) + 512].rearrange("p (b j s) -> p b j s", j=2, s=S)[:, :, j, :],
                ct[:, k, :].rearrange("p (b s) -> p b s", s=S)), t_ct) for k in range(KT) for j in range(2)]
            t_kv = []

            def context():
                for m in range(4):
                    b, ps, bfree = ringT.take()
                    for k in range(KT):
                        t = pe.op(lambda e, m=m, k=k, ps=ps: e.matmul(
                            ps[:, 0:256], wkv[0][:, k, 128 * m:128 * m + 128], ct[:, k, :], start=k == 0, stop=k == 3),
                            t_ct, t_wk, bfree, inc=k == 3)
                    for i in range(4):
                        r = slice(32 * i, 32 * i + 32)
                        src = ps[r, 0:256].rearrange("p (b s) -> p b s", s=S)
                        dh, dl = (q[r, :, m, 64 * i:64 * i + 64] for q in (kbh, kbl))
                        bias = cols[r, col_at["bk_c"] + m:col_at["bk_c"] + m + 1]
                        a = act.op(lambda e, dh=dh, src=src, bias=bias: e.activation(
                            dh, src, ACT.Identity, bias=bias, scale=1.0), t, tz, t_cols)
                        t_kv.append(dve.op(lambda e, dh=dh, dl=dl, src=src, bias=bias: e.scalar_tensor_tensor(
                            dl, src, bias, dh.bitcast(F32), ALU.add, ALU.subtract), a, tz))
                    ringT.free[b] = [a, t_kv[-1]]
                    yield 8
                t_wv = sp.dma(lane("wk"), wkv[0][:], A["Wv_c"].rearrange("(k p) n -> p k n", p=128), t)
                weight(0, "W2")
                for b in range(NB):
                    bk, ps, bfree = ringT.take()
                    for k in range(KT):
                        t = pe.op(lambda e, b=b, k=k, ps=ps: e.matmul(
                            ps, cd[k // 2][:, 512 * (k % 2) + 128 * b:512 * (k % 2) + 128 * b + 128], wkv[0][:, k, :],
                            start=k == 0, stop=k == 3), td, t_wv, bfree, inc=k == 3)
                    for j in range(2):
                        r = slice(64 * j, 64 * j + 64)
                        o, i0, i1 = (q.rearrange("p (h j d) -> p h j d", j=2, d=DH)[:, :, j, :]
                                     for q in (vb[r, b, :], ps[r, :], bvc[r, :]))
                        t_kv.append(dve.op(lambda e, o=o, i0=i0, i1=i1: e.tensor_tensor(o, i0, i1, ALU.add), t, tz, t_bvc))
                    ringT.free[bk] = [t_kv[-1]]
                    yield 16
                for i in range(2):
                    ppfree[i], pTfree[i] = [t], [t_kv[-1]]
                for i in range(4):
                    xfree[1][i] = rfree[0]
                    xfree[2][i] = rfree[1]

            ppfree, pTfree, cfree = [[], []], [[], []], [[], []]
            S_, P_, V_ = {}, {}, {}

            def scores(n):
                c, i = divmod(n, 4)
                b, qp, p = c // 2, c % 2, n % 2
                r = slice(128 * i, 128 * i + 128)
                b0, _, f0 = ringP.take()
                b1, _, f1 = ringP.take()
                for m in range(4):
                    ps = ringP.aps[b0 + m // 2][:, 256 * (m % 2):256 * (m % 2) + 256]
                    t = three(ps, (qh[qp][:, m, r], ql[qp][:, m, r]), (kbh[:, b, m, :], kbl[:, b, m, :]),
                              True, True, f0, f1, Q[c][m], t_kv)
                    yield 1.5
                if i == 3:
                    F["q"][qp] = [t]
                sc = psum[:, 3:5, :].rearrange("p a (h s) -> p (a h) s", s=S)
                t = dve.op(lambda e: e.tensor_reduce(nm_[p][:], sc, AX, ALU.max, negate=True), t)
                t = dve.op(lambda e: e.tensor_tensor(pp[p][:], sc, nm_[p][:].unsqueeze(2).broadcast_to((128, 16, S)),
                                                     ALU.add), t, ppfree[p])
                ringP.free[b0] = ringP.free[b1] = [t]
                S_[n] = act.op(lambda e: e.activation(pp[p][:], pp[p][:], ACT.Exp, scale=SCALE), t)

            def weights(n):
                p = n % 2
                t4 = dve.op(lambda e: e.tensor_reduce(sm_[p][:], pp[p][:], AX, ALU.add), S_[n])
                t5 = dve.op(lambda e: e.reciprocal(nm_[p][:], sm_[p][:]), t4)
                P_[n] = pool.op(lambda e: e.tensor_tensor(pp[p][:], pp[p][:], nm_[p][:].unsqueeze(2).broadcast_to((128, 16, S)),
                                                          ALU.mult), t5)

            def turn(n):
                p = n % 2
                V_[n] = []
                for hf in range(2):
                    bk, ps, bfree = ringT.take()
                    for u in range(4):
                        pr = 4 * hf + u
                        t = pe.op(lambda e, pr=pr, u=u, ps=ps: e.transpose(
                            ps[:, 128 * u:128 * u + 128], pp[p][:, 2 * pr:2 * pr + 2, :].rearrange("p h s -> p (h s)"),
                            ident[:]), P_[n], bfree, inc=u == 3)
                    a = act.op(lambda e, hf=hf, ps=ps: e.activation(
                        pT[p][:, 4 * hf:4 * hf + 4, :], ps.rearrange("p (u t) -> p u t", u=4), ACT.Copy), t, pTfree[p])
                    ringT.free[bk] = [a]
                    V_[n].append(a)
                    yield 2
                ppfree[p] = [t]

            C_ = {}

            def values(n):
                c, p = n // 4, n % 2
                b = c // 2
                bk, ps, bfree = ringT.take()
                for pr in range(8):
                    t = pe.op(lambda e, pr=pr, ps=ps: e.matmul(
                        ps[64 * (pr % 2):64 * (pr % 2) + 64, 128 * (pr // 2):128 * (pr // 2) + 128],
                        vb[:, b, 64 * pr:64 * pr + 64], pT[p][:, pr, :], start=True, stop=True),
                        V_[n], bfree, t_kv, inc=pr == 7)
                pTfree[p] = [t]
                pv = ps.rearrange("p (k t) -> p k t", k=4)
                a = act.op(lambda e, pv=pv: e.activation(ch[p][:], pv, ACT.Copy), t, cfree[p])
                C_[n] = dve.op(lambda e, pv=pv: e.tensor_tensor(cl[p][:], pv, ch[p][:].bitcast(F32), ALU.subtract), a, cfree[p])
                ringT.free[bk] = [a, C_[n]]
                yield 5

            def project(n):
                c, i = divmod(n, 4)
                p, px = n % 2, c % 3
                x = xt[px][:, i, :]
                bk, ps, bfree = ringT.take()
                for k in range(KT):
                    t = three(ps, (ch[p][:, k, :], cl[p][:, k, :]), (W["W2"][0][:, k, :], W["W2"][1][:, k, :]),
                              k == 0, k == 3, bfree, C_[n], tw["W2"])
                    yield 3
                cfree[p] = [t]
                d = dve.op(lambda e, ps=ps: e.tensor_tensor(x, ps, x, ALU.add), t, X[c][i])
                ringT.free[bk] = [d]
                xfree[px][i] = [sp.dma(lane(f"sx{px}{i}"), x2_d[128 * n:128 * n + 128, :], x, d)]

            def tiles(ns):
                for n in ns:
                    if n < 32:
                        yield from scores(n)
                    if 0 <= n - 3 < 32:
                        yield from project(n - 3)
                    if 0 <= n - 1 < 32:
                        yield from turn(n - 1)
                    if 0 <= n - 2 < 32:
                        yield from values(n - 2)
                    if n < 32:
                        weights(n)
                    yield 0.1

            merge((chunk(0), 115), (context(), 96))
            for c in range(8):
                merge((tiles(range(4 * c, 4 * c + 4)), 110), (chunk(c + 1) if c < 7 else iter(()), 115 + sum(CH_GAP)))
            for _ in tiles(range(32, 35)):
                pass
            fence()

        def phase3(ctx):
            f1h, f1l = (sb(ctx, f"f1{j}", [128, KT, 2048], F32R) for j in "hl")
            f2h, f2l = (sb(ctx, f"f2{j}", [128, 16, C], F32R) for j in "hl")
            xt = [sb(ctx, f"fx{p}", [128, 2, C]) for p in range(2)]
            xn_ = [sb(ctx, f"fn{p}", [128, 2, C]) for p in range(2)]
            ah = [sb(ctx, f"fah{p}", [128, KT, 256], F32R) for p in range(2)]
            al = [sb(ctx, f"fal{p}", [128, KT, 256], F32R) for p in range(2)]
            hh = [[sb(ctx, f"hh{p}{q}", [128, 4, 256], F32R) for q in range(2)] for p in range(2)]
            hl = [[sb(ctx, f"hl{p}{q}", [128, 4, 256], F32R) for q in range(2)] for p in range(2)]
            yb = [sb(ctx, f"fy{p}", [128, 512]) for p in range(2)]
            y2 = [[yb[p][:, 256 * i:256 * i + 256] for i in range(2)] for p in range(2)]
            bfb = sb(ctx, "bfb", [128, C])
            t_bf = sp.dma(lane("bf"), bfb[:], A["bf2"].partition_broadcast(128))
            raw = [sb(ctx, f"fw{i}", [128, 1024])[:] for i in range(NRAW)]
            rf = [[] for _ in raw]
            tw1, tw2 = {}, {}

            def weights3():
                parts = [(0, k, 0) for k in range(4)] + [(1, 0, 0), (1, 1, 0)] + [(0, k, 1) for k in range(4)]
                parts += [(1, u, 0) for u in range(2, 8)]
                for n, (kind, u, hf) in enumerate(parts):
                    j = n % NRAW
                    if kind == 0:
                        src = A["Wf1"][128 * u:128 * u + 128, 1024 * hf:1024 * hf + 1024]
                        rr = raw[j]
                        hi, lo = (q[:, u, 1024 * hf:1024 * hf + 1024] for q in (f1h, f1l))
                    else:
                        src = A["Wf2"][256 * u:256 * u + 256, :].rearrange("(k p) n -> p k n", p=128)
                        rr = raw[j].rearrange("p (k n) -> p k n", k=2)
                        hi, lo = (q[:, 2 * u:2 * u + 2, :] for q in (f2h, f2l))
                    t = sp.dma(lane(f"fr{j}"), rr, src, rf[j])
                    a = act.op(lambda e, hi=hi, rr=rr: e.activation(hi, rr, ACT.Copy), t)
                    d = dve.op(lambda e, hi=hi, lo=lo, rr=rr: e.tensor_tensor(lo, rr, hi.bitcast(F32), ALU.subtract), t, a)
                    rf[j] = [a, d]
                    if kind == 0:
                        tw1[u, hf] = d
                    else:
                        tw2[u] = d
                    yield

            wvb = [sb(ctx, f"wvb{i}", [128, C]) for i in range(2)]
            t_wvb = {b: sp.dma(lane(f"wvb{b}"), wvb[b][:], wvp_d[b, :].partition_broadcast(128)) for b in range(2)}
            t_cb = sp.dma(lane("cbb"), cb[:], cb_d.rearrange("b a -> (b a)").partition_broadcast(128))
            agt = {}

            def route(b):
                d = dve.op(lambda e: e.tensor_scalar(ag[:, b, :], ag[:, b, :], cb[:, b:b + 1], 2.0, ALU.add, ALU.mult),
                           agt[b], t_cb)
                d = dve.op(lambda e: e.tensor_reduce(sm4[:, b, 0:1], ag[:, b, :], AX, ALU.max), d)
                p = pool.op(lambda e: e.partition_all_reduce(sm4[:, b, 1:2], sm4[:, b, 0:1], 128, bass.bass_isa.ReduceOp.max), d)
                d = dve.op(lambda e: e.tensor_scalar(sm4[:, b, 2:3], sm4[:, b, 1:2], -1.0, None, ALU.mult), p)
                a = act.op(lambda e: e.activation(rw[:, b, :], ag[:, b, :], ACT.Exp, bias=sm4[:, b, 2:3], scale=1.0,
                                                  accum_out=sm4[:, b, 3:4]), d)
                p = pool.op(lambda e: e.partition_all_reduce(sm4[:, b, 4:5], sm4[:, b, 3:4], 128, bass.bass_isa.ReduceOp.add), a)
                d = dve.op(lambda e: e.reciprocal(sm4[:, b, 5:6], sm4[:, b, 4:5]), p)
                R["rw", b] = dve.op(lambda e: e.tensor_scalar(rw[:, b, :], rw[:, b, :], sm4[:, b, 5:6], None, ALU.mult), d, a)

            accs = [Banks(bank[0:2]), Banks(bank[4:6])]
            rings = [Banks(bank[2:4]), Banks(bank[6:8])]
            F = [{"x": [[], []], "n": [], "a": [], "h": [[], []], "y": [[], []], "yb": []} for p in range(2)]

            def chunk3(c):
                p = c % 2
                f, ring = F[p], rings[p]
                t0 = 256 * c
                xs = [xt[p][:, i, :] for i in range(2)]
                xn = [xn_[p][:, i, :] for i in range(2)]
                tx = [sp.dma(lane(f"fx{p}{i}"), xs[i], x2_d[t0 + 128 * i:t0 + 128 * i + 128, :], f["x"][i]) for i in range(2)]
                yield
                mv, r_, tr = layer_stats(xs, tx, small[:, p, :])
                yield
                dve.wait(f["n"])
                tn = normalise(xs, xn, tx, mv, r_, tr)
                tb = [pool.op(lambda e, i=i: e.tensor_tensor(xs[i], xs[i], bfb[:], ALU.add), tn[i], t_bf) for i in range(2)]
                yield
                for step in transposed(xn, tn, ring, y2[p], f["y"], "g3", "be3", ah[p], al[p], f["a"]):
                    if step is None:
                        yield
                    else:
                        txn, tl = step
                f["n"] = [tl]
                f["yb"] = f["y"][0] + f["y"][1]
                acc = [accs[p].take() for _ in range(2)]
                prev = None
                for qd in range(5):
                    if qd < 4:
                        th = []
                        hb = qd % 2
                        for m2 in range(2):
                            bk, ps, bfree = ring.take()
                            ty = []
                            for u in range(2):
                                m = 4 * qd + 2 * m2 + u
                                for k in range(KT):
                                    t = three(ps[:, 256 * u:256 * u + 256],
                                              tuple(q[:, k, 128 * m:128 * m + 128] for q in (f1h, f1l)),
                                              (ah[p][:, k, :], al[p][:, k, :]), k == 0, k == 3, bfree, txn[k],
                                              tw1[k, m // 8])
                            for u in range(2):
                                m = 4 * qd + 2 * m2 + u
                                ty.append(act.op(lambda e, u=u, m=m, ps=ps: e.activation(
                                    yb[p][:, 256 * u:256 * u + 256], ps[:, 256 * u:256 * u + 256], ACT.Relu,
                                    bias=col("bf1", m), scale=1.0), t, f["yb"]))
                            ring.free[bk] = [ty[-1]]
                            yv = yb[p][:].rearrange("p (m t) -> p m t", m=2)
                            hi, lo = (q[p][hb][:, 2 * m2:2 * m2 + 2, :] for q in (hh, hl))
                            a = dve.op(lambda e, hi=hi, yv=yv: e.tensor_copy(hi, yv), ty, f["h"][hb])
                            d = dve.op(lambda e, hi=hi, lo=lo, yv=yv: e.tensor_tensor(lo, yv, hi.bitcast(F32), ALU.subtract), a)
                            f["yb"] = [d]
                            th.append(d)
                            yield
                        if qd == 3:
                            f["a"] = [t]
                        cur = (qd, hb, th)
                    else:
                        cur = None
                    if prev:
                        q0, hb, th = prev
                        for i in range(2):
                            ab, ps, afree = acc[i]
                            for m in range(4):
                                r = slice(128 * i, 128 * i + 128)
                                t = three(ps, (hh[p][hb][:, m, r], hl[p][hb][:, m, r]),
                                          (f2h[:, 4 * q0 + m, :], f2l[:, 4 * q0 + m, :]), q0 == 0 and m == 0, q0 == 3 and m == 3,
                                          afree, th[m // 2], tw2[2 * q0 + m // 2])
                            if q0 < 3 and i == 1:
                                pe.items[-1] = (pe.items[-1][0], pe.sem, 1)
                                pe.n += 1
                                t = pe.last()
                            if q0 == 3:
                                d = dve.op(lambda e, i=i, ps=ps: e.tensor_tensor(xs[i], ps, xs[i], ALU.add), t, tb[i])
                                accs[p].free[ab] = [d]
                                b, tt = divmod(2 * c + i, 8)
                                g = dve.op(lambda e, i=i, b=b, tt=tt: e.tensor_tensor_reduce(
                                    out=xn[i], in0=xs[i], in1=wvb[b % 2][:], scale=1.0, scalar=0.0, op0=ALU.mult,
                                    op1=ALU.add, accum_out=ag[:, b, tt:tt + 1]), d, t_wvb[b], agt.get(b))
                                agt[b] = g
                                if tt == 7:
                                    if b + 2 < NB:
                                        t_wvb[b + 2] = sp.dma(lane(f"wvb{b + 2}"), wvb[b % 2][:],
                                                              wvp_d[b + 2, :].partition_broadcast(128), g)
                                    route(b)
                                f["x"][i] = [sp.dma(lane(f"fs{p}{i}"), x3_d[t0 + 128 * i:t0 + 128 * i + 128, :], xs[i], d), g]
                            yield
                        f["h"][hb] = [t]
                    prev = cur
                f["y"] = [list(f["yb"]), list(f["yb"])]

            def first():
                w = weights3()
                for n, _ in enumerate(chunk3(0)):
                    if n >= W_AT:
                        next(w, None)
                        next(w, None)
                    yield

            window([first()] + [chunk3(c) for c in range(1, 16)], 8)
            fence()

        def phase4(ctx):
            wh = sb(ctx, "wh4", [128, KT, C], F32R)
            wl = sb(ctx, "wl4", [128, KT, C], F32R)
            vpb = sb(ctx, "vpb", [128, NB, C])
            ub = sb(ctx, "ub", [128, NB, C])
            gb = sb(ctx, "gb", [128, C])
            rows = sb(ctx, "rows4", [128, 2, C])
            NX, NG = 16, 16
            x3 = [sb(ctx, f"x3{i}", [128, C]) for i in range(NX)]
            th_ = [sb(ctx, f"th{p}", [128, KT, 128], F32R) for p in range(4)]
            tl_ = [sb(ctx, f"tl{p}", [128, KT, 128], F32R) for p in range(4)]
            gt = [sb(ctx, f"gt{p}", [128, C]) for p in range(NG)]

            x3free = [[] for _ in range(NX)]
            X = {}

            def load(n):
                X[n] = sp.dma(lane(f"g{n % NX}"), x3[n % NX][:], x3_d[128 * n:128 * n + 128, :], x3free[n % NX])

            for n in range(4):
                load(n)
            t_w = [sp.dma(lane(f"w4{j}"), (wh, wl)[j][:].bitcast(F32), (wh_d, wl_d)[j].rearrange("(k p) n -> p k n", p=128))
                   for j in range(2)]
            t_ub = [sp.dma(lane("ub"), ub[:, b, :], u_d[b, :].partition_broadcast(128)) for b in range(NB)][-1]
            t_gb = sp.dma(lane("gb4"), gb[:], gb_d[0, :].partition_broadcast(128))
            t_vp = [sp.dma(lane("vpb"), vpb[:, b, :], vp_d[b, :].partition_broadcast(128)) for b in range(NB)][-1]
            t_row = [sp.dma(lane("rows4"), rows[:, j, :], A[nm].partition_broadcast(128))
                     for j, nm in enumerate(("gamma", "beta"))][-1]
            for n in range(4, NX):
                load(n)
            ring = Banks(bank)
            tfree = [[] for _ in range(4)]
            gfree = [[] for _ in range(NG)]

            ready = {}

            def fuse(n):
                b = n // 8
                x, g, h = x3[n % NX], gt[n % NG], n % 4
                bk, ps, bfree = ring.take()
                for k in range(KT):
                    t = pe.op(lambda e, k=k: e.transpose(ps[:, 128 * k:128 * k + 128], x[:, 128 * k:128 * k + 128], ident[:]),
                              bfree, X[n], inc=k == 3)
                pv = ps.rearrange("p (k t) -> p k t", k=4)
                a = act.op(lambda e: e.activation(th_[h][:], pv, ACT.Copy), t, tfree[h])
                yield
                d = dve.op(lambda e: e.tensor_tensor(tl_[h][:], pv, th_[h][:].bitcast(F32), ALU.subtract), a, tfree[h])
                ring.free[bk] = [a, d]
                yield
                bk, ps2, bfree = ring.take()
                for k in range(KT):
                    t = three(ps2, (th_[h][:, k, :], tl_[h][:, k, :]), (wh[:, k, :], wl[:, k, :]), k == 0, k == 3,
                              bfree, d, t_w)
                tfree[h] = [t]
                yield
                r = rw[:, b, n % 8:n % 8 + 1]
                d = dve.op(lambda e: e.scalar_tensor_tensor(g[:], ub[:, b, :], r, ps2, ALU.mult, ALU.add),
                           t, R["rw", b], t_ub, gfree[n % NG])
                ring.free[bk] = [d]
                d = pool.op(lambda e: e.tensor_tensor(g[:], g[:], gb[:], ALU.add), d, t_gb)
                yield
                yield
                d = act.op(lambda e: e.activation(g[:], g[:], ACT.Sigmoid), d)
                d = pool.op(lambda e: e.tensor_tensor(g[:], g[:], vpb[:, b, :], ALU.mult), d, t_vp)
                yield
                yield
                d = dve.op(lambda e: e.scalar_tensor_tensor(g[:], g[:], r, x[:], ALU.mult, ALU.add), d)
                x3free[n % NX] = [d, t]
                if n + NX < 32:
                    load(n + NX)
                ready[n] = d
                if n % 4 == 3:
                    yield
                    gs = [gt[m % NG][:] for m in range(n - 3, n + 1)]
                    toks = [ready[m] for m in range(n - 3, n + 1)]
                    mv, r_, tr = layer_stats(gs, toks, small[:, (n // 4) % 2, :])
                    tn = normalise(gs, gs, toks, mv, r_, tr)
                    yield
                    for i in range(4):
                        p = pool.op(lambda e, i=i: e.tensor_tensor(gs[i], gs[i], rows[:, 0, :], ALU.mult), tn[i], t_row)
                        ready[n - 3 + i] = p
                        if i:
                            last(n - 4 + i)
                        yield
                    last(n)

            def last(n):
                g = gt[n % NG]
                d = dve.op(lambda e: e.tensor_tensor(g[:], g[:], rows[:, 1, :], ALU.add), ready[n])
                gfree[n % NG] = [sp.dma(lane(f"o{n % NG}"), out_d[128 * n:128 * n + 128, :], g[:], d)]

            window([fuse(n) for n in range(32)], 1, 16)
            sp.wait([(l[0], l[1]) for l in lanes.values()])

        for phase in (phase0, phase1, phase2, phase3, phase4):
            with ExitStack() as ctx:
                phase(ctx)

        block = top.enter_context(nc.Block())

        @block.tensor
        def _(e):
            pe.play(e)

        @block.scalar
        def _(e):
            act.play(e)

        @block.vector
        def _(e):
            dve.play(e)

        @block.gpsimd
        def _(e):
            pool.play(e)

        @block.sync
        def _(e):
            sp.play(e)


def kernel(**inputs):
    import numpy as _np
    import concourse.bacc as _bacc
    from concourse import mybir as _mybir
    from concourse.bass_utils import run_bass_kernel_spmd as _run

    f = {k[9:] if k.startswith("L") else k: _np.asarray(a) for k, a in inputs.items() if not k.startswith("L1")}
    g = {k[9:]: _np.asarray(a) for k, a in inputs.items() if k.startswith("L1")}
    heads = lambda w: w.transpose(1, 0, 2).reshape(512, 512)
    column = lambda v: v.reshape(-1, 128).T
    lay = {"x": f["x"], "ctxT": f["ctx_1024"].reshape(256, 512).T}
    stacked = lambda w: w.reshape(-1, 4, 4, 32).transpose(0, 1, 3, 2).reshape(-1, 512)
    for s in "sc":
        for n in "qkv":
            lay[f"W{n}_{s}"] = heads(f[f"W{n}_{s}"])
            lay[f"b{n}_{s}"] = f[f"b{n}_{s}"].reshape(512)
    for n in "qk":
        lay[f"W{n}_s"] = stacked(lay[f"W{n}_s"])
        lay[f"b{n}_s"] = stacked(lay[f"b{n}_s"])
    for n in ("bq_s", "bk_s", "bv_s", "bq_c", "bk_c"):
        lay[n] = column(lay[n])
    for n in ("g1", "be1", "g2", "be2", "g3", "be3", "bf1"):
        lay[n] = column(f[n])
    for n in ("W1", "W2", "Wf1", "Wf2", "b1", "b2", "bf2"):
        lay[n] = f[n]
    lay["bt"], lay["bv1"], lay["bv1r"] = column(g["bt"]), column(g["bv"]), g["bv"]
    lay["Wt"], lay["Wv1"], lay["Wg"] = g["Wt"], g["Wv"].T, g["Wg"].T
    for n in ("bg", "gamma", "beta"):
        lay[n] = g[n]

    nc = _bacc.Bacc("TRN2", target_bir_lowering=False, num_devices=1, dynamic_dma_scratch_size=1024)
    arrays, aps = {}, {}
    for n, a in lay.items():
        a = _np.ascontiguousarray(a)
        arrays[f"in_{n}"] = a
        aps[n] = nc.dram_tensor(f"in_{n}", a.shape, _mybir.dt.from_np(a.dtype), kind="ExternalInput").ap()
    out = nc.dram_tensor("out_0", (4, 1024, 512), _mybir.dt.float32, kind="ExternalOutput").ap()
    program(nc, aps, out)
    r = _run(nc, [arrays], core_ids=[0])
    return r.results[0]["out_0"]
```
